# Optimizing a Trainium2 kernel written in Bass

```python
import numpy as np
import jax
import jax.numpy as jnp

def _softmax(x, axis=-1):
    return jax.nn.softmax(x, axis=axis)

def _gelu(x):
    return jax.nn.gelu(x, approximate=True)

def _silu(x):
    return jax.nn.silu(x)

def _sigmoid(x):
    return jax.nn.sigmoid(x)

def _layernorm(x, axis=-1, eps=1e-05):
    m = jnp.mean(x, axis=axis, keepdims=True)
    v = jnp.var(x, axis=axis, keepdims=True)
    return (x - m) / jnp.sqrt(v + eps)

def _scatter_add(tgt, idx, src, axis=0):
    return tgt.at[idx].add(src)

def _segment_sum(src, seg, n):
    return jax.ops.segment_sum(src, seg, n)
kernel_name = 'mk_recurrent_d2_jaxref_r8_e3209c'

def setup_inputs(seed: int=0):
    np.random.seed(seed)
    _w = jnp.asarray

    def _L0_attn_setup():
        import jax, jax.numpy as jnp
        import numpy as np
        import math
        DIM_EMB = 128
        DIM_QK = 128
        DIM_V = 128
        NORM_FACT = 1.0 / math.sqrt(DIM_EMB)
        key = jax.random.key(seed)
        k0, k1, k2, k3 = jax.random.split(key, 4)
        x = jax.random.normal(k0, (4, 512, DIM_EMB), dtype=jnp.float32)
        s = 1.0 / math.sqrt(DIM_EMB)
        Wq = jax.random.uniform(k1, (DIM_QK, DIM_EMB), jnp.float32, -s, s)
        Wk = jax.random.uniform(k2, (DIM_QK, DIM_EMB), jnp.float32, -s, s)
        Wv = jax.random.uniform(k3, (DIM_V, DIM_EMB), jnp.float32, -s, s)
        return {'x': x, 'Wq': Wq, 'Wk': Wk, 'Wv': Wv}
    _L0_attn_in = _L0_attn_setup()

    def _L0_ffn_setup():
        import jax, jax.numpy as jnp
        import numpy as np
        B, S, H, F, G = (8, 256, 128, 512, 128)
        EPS = 1e-05

        def _dequant(q, scales, g):
            K, N = q.shape
            w = (q.astype(jnp.float32) - 128.0).reshape(K // g, g, N) * scales[:, None, :]
            return w.reshape(K, N)
        key = jax.random.key(seed)
        ks = jax.random.split(key, 8)
        x = jax.random.normal(ks[0], (B, S, H), dtype=jnp.float32)
        ln_gamma = jnp.ones((H,), jnp.float32)
        ln_beta = jnp.zeros((H,), jnp.float32)
        fc1_q = jax.random.randint(ks[1], (H, F), 0, 32, dtype=jnp.int32)
        fc2_q = jax.random.randint(ks[2], (F, H), 0, 32, dtype=jnp.int32)
        fc1_scales = jax.random.uniform(ks[3], (H // G, F), jnp.float32) * 0.02 + 0.001
        fc2_scales = jax.random.uniform(ks[4], (F // G, H), jnp.float32) * 0.02 + 0.001
        fc1_bias = jax.random.normal(ks[5], (F,), jnp.float32) * 0.02
        fc2_bias = jax.random.normal(ks[6], (H,), jnp.float32) * 0.02
        return {'x': x, 'ln_gamma': ln_gamma, 'ln_beta': ln_beta, 'fc1_q': fc1_q, 'fc1_scales': fc1_scales, 'fc1_bias': fc1_bias, 'fc2_q': fc2_q, 'fc2_scales': fc2_scales, 'fc2_bias': fc2_bias}
    _L0_ffn_in = _L0_ffn_setup()

    def _L1_attn_setup():
        import jax, jax.numpy as jnp
        import numpy as np
        NUM_HEADS = 16
        key = jax.random.key(seed)
        k1, k2, k3 = jax.random.split(key, 3)
        S, B, E = (256, 4, 128)
        std = float(np.sqrt(2.0 / (E + E)))
        query = jax.random.normal(k1, (S, B, E), dtype=jnp.float32)
        in_proj_weight = jax.random.normal(k2, (3 * E, E), dtype=jnp.float32) * std
        in_proj_bias = jnp.zeros((3 * E,), dtype=jnp.float32)
        out_proj_weight = jax.random.normal(k3, (E, E), dtype=jnp.float32) * std
        out_proj_bias = jnp.zeros((E,), dtype=jnp.float32)
        return {'query': query, 'in_proj_weight': in_proj_weight, 'in_proj_bias': in_proj_bias, 'out_proj_weight': out_proj_weight, 'out_proj_bias': out_proj_bias}
    _L1_attn_in = _L1_attn_setup()

    def _L1_ffn_setup():
        import jax, jax.numpy as jnp
        import numpy as np
        B, S, H, E, I, K = (2, 256, 128, 8, 128, 2)
        ALPHA, LIMIT = (1.702, 7.0)
        key = jax.random.key(seed)
        ks = jax.random.split(key, 5)
        sc = 0.02
        return {'hidden_states': jax.random.normal(ks[0], (B, S, H), jnp.float32), 'router_weight': jax.random.normal(ks[1], (H, E), jnp.float32) * sc, 'gate_up_proj': jax.random.normal(ks[2], (E, H, 2 * I), jnp.float32) * sc, 'gate_up_proj_bias': jnp.zeros((E, 2 * I), jnp.float32), 'down_proj': jax.random.normal(ks[3], (E, I, H), jnp.float32) * sc, 'down_proj_bias': jnp.zeros((E, H), jnp.float32)}
    _L1_ffn_in = _L1_ffn_setup()
    _d = {'L0_attn_x': _L0_attn_in['x'], 'L0_attn_Wq': _L0_attn_in['Wq'], 'L0_attn_Wk': _L0_attn_in['Wk'], 'L0_attn_Wv': _L0_attn_in['Wv'], 'L0_ffn_ln_gamma': _L0_ffn_in['ln_gamma'], 'L0_ffn_ln_beta': _L0_ffn_in['ln_beta'], 'L0_ffn_fc1_q': _L0_ffn_in['fc1_q'], 'L0_ffn_fc1_scales': _L0_ffn_in['fc1_scales'], 'L0_ffn_fc1_bias': _L0_ffn_in['fc1_bias'], 'L0_ffn_fc2_q': _L0_ffn_in['fc2_q'], 'L0_ffn_fc2_scales': _L0_ffn_in['fc2_scales'], 'L0_ffn_fc2_bias': _L0_ffn_in['fc2_bias'], 'L1_attn_in_proj_weight': _L1_attn_in['in_proj_weight'], 'L1_attn_in_proj_bias': _L1_attn_in['in_proj_bias'], 'L1_attn_out_proj_weight': _L1_attn_in['out_proj_weight'], 'L1_attn_out_proj_bias': _L1_attn_in['out_proj_bias'], 'L1_ffn_router_weight': _L1_ffn_in['router_weight'], 'L1_ffn_gate_up_proj': _L1_ffn_in['gate_up_proj'], 'L1_ffn_gate_up_proj_bias': _L1_ffn_in['gate_up_proj_bias'], 'L1_ffn_down_proj': _L1_ffn_in['down_proj'], 'L1_ffn_down_proj_bias': _L1_ffn_in['down_proj_bias']}
    _x0 = _d['L0_attn_x']
    _d['L0_attn_x'] = jax.random.normal(jax.random.fold_in(jax.random.key(seed), 1), (2, 1024, 128), dtype=_x0.dtype)
    del _x0
    return _d

def reference(L0_attn_x, L0_attn_Wq, L0_attn_Wk, L0_attn_Wv, L0_ffn_ln_gamma, L0_ffn_ln_beta, L0_ffn_fc1_q, L0_ffn_fc1_scales, L0_ffn_fc1_bias, L0_ffn_fc2_q, L0_ffn_fc2_scales, L0_ffn_fc2_bias, L1_attn_in_proj_weight, L1_attn_in_proj_bias, L1_attn_out_proj_weight, L1_attn_out_proj_bias, L1_ffn_router_weight, L1_ffn_gate_up_proj, L1_ffn_gate_up_proj_bias, L1_ffn_down_proj, L1_ffn_down_proj_bias):

    def _L0_attn_ref(x, Wq, Wk, Wv):
        import jax, jax.numpy as jnp
        import numpy as np
        import math
        DIM_EMB = 128
        DIM_QK = 128
        DIM_V = 128
        NORM_FACT = 1.0 / math.sqrt(DIM_EMB)
        q = jnp.einsum('bne,de->bnd', x, Wq)
        k = jnp.einsum('bne,de->bnd', x, Wk)
        v = jnp.einsum('bne,de->bnd', x, Wv)
        logits = jnp.einsum('bnd,bmd->bnm', q, k)
        score = jax.nn.softmax(logits, axis=-1) * NORM_FACT
        att = jnp.einsum('bnm,bmv->bnv', score, v)
        return att

    def _L0_ffn_ref(x, ln_gamma, ln_beta, fc1_q, fc1_scales, fc1_bias, fc2_q, fc2_scales, fc2_bias):
        import jax, jax.numpy as jnp
        import numpy as np
        B, S, H, F, G = (8, 256, 128, 512, 128)
        EPS = 1e-05

        def _dequant(q, scales, g):
            K, N = q.shape
            w = (q.astype(jnp.float32) - 128.0).reshape(K // g, g, N) * scales[:, None, :]
            return w.reshape(K, N)
        residual = x
        mu = jnp.mean(x, axis=-1, keepdims=True)
        var = jnp.mean(jnp.square(x - mu), axis=-1, keepdims=True)
        h = (x - mu) * jax.lax.rsqrt(var + EPS) * ln_gamma + ln_beta
        hf = h.reshape(-1, H)
        w1 = _dequant(fc1_q, fc1_scales, G)
        y = hf @ w1 + fc1_bias
        y = jax.nn.silu(y)
        w2 = _dequant(fc2_q, fc2_scales, G)
        z = y @ w2 + fc2_bias
        return residual + 0.5 * z.reshape(residual.shape)

    def _L1_attn_ref(query, in_proj_weight, in_proj_bias, out_proj_weight, out_proj_bias):
        import jax, jax.numpy as jnp
        import numpy as np
        NUM_HEADS = 16
        S, B, E = query.shape
        H = NUM_HEADS
        hd = E // H
        scale = hd ** (-0.5)
        lin = jnp.einsum('sbe,fe->sbf', query, in_proj_weight) + in_proj_bias
        lin = lin.reshape(S, B * H, 3, hd)
        q = lin[:, :, 0, :]
        k = lin[:, :, 1, :]
        v = lin[:, :, 2, :]
        scores = jnp.einsum('sbd,tbd->bst', q, k) * scale
        attn = jax.nn.softmax(scores.astype(jnp.float32), axis=-1).astype(scores.dtype)
        ctx = jnp.einsum('bst,tbd->sbd', attn, v).reshape(S, B, E)
        out = jnp.einsum('sbe,fe->sbf', ctx, out_proj_weight) + out_proj_bias
        return out

    def _L1_ffn_ref(hidden_states, router_weight, gate_up_proj, gate_up_proj_bias, down_proj, down_proj_bias):
        import jax, jax.numpy as jnp
        import numpy as np
        B, S, H, E, I, K = (2, 256, 128, 8, 128, 2)
        ALPHA, LIMIT = (1.702, 7.0)
        Bt, St, Ht = hidden_states.shape
        x = hidden_states.reshape(-1, Ht)
        T = x.shape[0]
        logits = x @ router_weight
        top_vals, top_idx = jax.lax.top_k(logits, K)
        scores = jax.nn.softmax(top_vals, axis=-1)
        w = jnp.zeros((T, E), x.dtype).at[jnp.arange(T)[:, None], top_idx].set(scores)
        gu = jnp.einsum('th,ehf->tef', x, gate_up_proj) + gate_up_proj_bias
        gate = gu[..., ::2]
        up = gu[..., 1::2]
        gate = jnp.minimum(gate, LIMIT)
        up = jnp.clip(up, -LIMIT, LIMIT)
        glu = gate * jax.nn.sigmoid(gate * ALPHA)
        act = (up + 1.0) * glu
        down = jnp.einsum('tei,eih->teh', act, down_proj) + down_proj_bias
        out = jnp.einsum('te,teh->th', w, down)
        return out.reshape(Bt, St, Ht)
    x = L0_attn_x
    xn = _layernorm(x, axis=-1)
    s = _L0_attn_ref(xn, L0_attn_Wq, L0_attn_Wk, L0_attn_Wv)
    g = _silu(_L0_ffn_ref(xn, L0_ffn_ln_gamma, L0_ffn_ln_beta, L0_ffn_fc1_q, L0_ffn_fc1_scales, L0_ffn_fc1_bias, L0_ffn_fc2_q, L0_ffn_fc2_scales, L0_ffn_fc2_bias))
    x = x + s * g
    xn = _layernorm(x, axis=-1)
    s = _L1_attn_ref(xn, L1_attn_in_proj_weight, L1_attn_in_proj_bias, L1_attn_out_proj_weight, L1_attn_out_proj_bias)
    g = _silu(_L1_ffn_ref(xn, L1_ffn_router_weight, L1_ffn_gate_up_proj, L1_ffn_gate_up_proj_bias, L1_ffn_down_proj, L1_ffn_down_proj_bias))
    x = x + s * g
    return x

_drawn_inputs = setup_inputs


def setup_inputs(seed=0):
    import zlib

    import numpy as np

    out = dict(_drawn_inputs(seed))
    spreads = {'L0_ffn_ln_gamma': (1.0, 0.2),
     'L0_ffn_ln_beta': (0.0, 0.1),
     'L1_attn_in_proj_bias': (0.0, 0.8),
     'L1_attn_out_proj_bias': (0.0, 0.8),
     'L1_ffn_gate_up_proj_bias': (0.0, 0.8),
     'L1_ffn_down_proj_bias': (0.0, 0.317)}
    factors = {'L0_ffn_fc1_bias': 8.0,
     'L0_ffn_fc2_bias': 8.0,
     'L1_ffn_gate_up_proj': 8.0,
     'L1_ffn_down_proj': 7.788}
    for name, (base, spread) in spreads.items():
        noise = np.random.default_rng([zlib.crc32(name.encode()), seed]).standard_normal(out[name].shape)
        drawn = base * np.exp(spread * noise) if base else spread * noise
        out[name] = jnp.asarray(drawn.astype(out[name].dtype))
    for name, factor in factors.items():
        out[name] = (out[name] * factor).astype(out[name].dtype)
    return out
```

```python
from contextlib import ExitStack

import concourse.bass as bass
from concourse import mybir

P = 128
TOKENS = 2048
TILES = TOKENS // P
BATCHES = 2
BT = TILES // BATCHES
KEYS = TOKENS // BATCHES
CHUNK = 512
CHUNKS = TOKENS // CHUNK
CT = CHUNK // P
FFN = 512
FB = FFN // P
EXPERTS = 8
HEADS = 16
HD = P // HEADS
EPS = 1e-5
NORM_FACT = float(P) ** -0.5
HEAD_SCALE = float(HD) ** -0.5
ZERO_POINT = 128.0
ALPHA, LIMIT = 1.702, 7.0
RSQRT_MAGIC = float(0x5F3759DF)
LOWEST = -3.0e38

GAMMA, BETA, FC1B, BQ, BV, BO, GB = 0, 1, 2, 6, 7, 8, 9
UB = GB + EXPERTS
VECS = UB + EXPERTS
WQ, WK, WVT = 0, 1, 2
IQ, IK, IV, OUT = 0, 1, 2, 3


def build(nc, x, w0, w1s, vecs, q1, q2, s1, s2, b2, gup, down, db, out):
    f32, f16, i32 = mybir.dt.float32, mybir.dt.float16, mybir.dt.int32
    ALU = mybir.AluOpType
    ACT = mybir.ActivationFunctionType
    AX = mybir.AxisListType
    ds = bass.ds

    x_rows = x.rearrange("(t p) d -> p t d", p=P)
    out_rows = out.rearrange("(t p) d -> p t d", p=P)

    ctx = ExitStack()
    with ctx:
        def sb(name, shape, dt=f32):
            return ctx.enter_context(nc.sbuf_tensor(name, shape, dt))

        def sem(name):
            return ctx.enter_context(nc.semaphore(name))

        ident = sb("ident", [P, P])
        ident16 = sb("ident16", [P, P], f16)
        headsum = sb("headsum", [P, P])
        sel16 = sb("sel16", [2 * EXPERTS, EXPERTS, P], f16)
        rank = sb("rank", [P, EXPERTS])

        x_sb = sb("x_sb", [P, TILES, P])
        xn = sb("xn", [P, TILES, P])
        hz = sb("hz", [P, TILES, P])
        xnb = sb("xnb", [P, TILES, P])
        gate0 = sb("gate0", [P, TILES, P])
        xT_hi = sb("xT_hi", [P, TOKENS], f16)
        xT_lo = sb("xT_lo", [P, TOKENS], f16)
        hT32 = sb("hT32", [P, 2, CHUNK])
        hT_hi = sb("hT_hi", [P, TOKENS], f16)
        hT_lo = sb("hT_lo", [P, TOKENS], f16)
        kT_hi = sb("kT_hi", [P, TOKENS], f16)
        kT_lo = sb("kT_lo", [P, TOKENS], f16)
        v_hi = sb("v_hi", [P, TILES, P], f16)
        v_lo = sb("v_lo", [P, TILES, P], f16)
        yT = sb("yT", [P, FB, CHUNK])
        u0 = sb("u0", [P, 2, CHUNK])
        probs = sb("probs", [P, 2, KEYS])
        pT_hi = sb("pT_hi", [P, KEYS], f16)
        pT_lo = sb("pT_lo", [P, KEYS], f16)
        sg0 = sb("sg0", [P, 2, P])
        x1 = hz

        stats = sb("stats", [P, TILES, 6])
        mv = sb("mv", [P, TILES, 2])
        stats1 = sb("stats1", [P, TILES, 6])
        mv1 = sb("mv1", [P, TILES, 2])
        var_e = sb("var_e", [P, TILES])
        rstd = sb("rstd", [P, TILES])
        rstd2 = sb("rstd2", [P, TILES])
        rstd1 = sb("rstd1", [P, TILES])
        half_a = sb("half_a", [P, TILES])
        seed = sb("seed", [P, TILES], i32)
        newt = sb("newt", [P, TILES])
        newt2 = sb("newt2", [P, TILES])
        neg_max = sb("neg_max", [P, TILES])
        row_sum = sb("row_sum", [P, TILES])
        row_inv = sb("row_inv", [P, TILES])

        w0_sb = sb("w0_sb", [P, 3, P])
        A_hi = sb("A_hi", [P, P], f16)
        A_lo = sb("A_lo", [P, P], f16)
        wv_hi = sb("wv_hi", [P, P], f16)
        wv_lo = sb("wv_lo", [P, P], f16)
        vecs_sb = sb("vecs_sb", [P, VECS])
        ub1 = sb("ub1", [P, EXPERTS])
        q1_sb = sb("q1_sb", [P, FFN], i32)
        q2_sb = sb("q2_sb", [P, FB, P], i32)
        s1_sb = sb("s1_sb", [P, FFN])
        s2_sb = sb("s2_sb", [P, FB, P])
        b2_sb = sb("b2_sb", [P, P])
        fc1_w = sb("fc1_w", [P, FFN])
        fc1_hi = sb("fc1_hi", [P, FFN], f16)
        fc1_lo = sb("fc1_lo", [P, FFN], f16)
        fc2_w = sb("fc2_w", [P, FB, P])

        W1COLS = 4 * P + EXPERTS
        w1_sb = sb("w1_sb", [P, W1COLS])
        w1_hi = sb("w1_hi", [P, W1COLS], f16)
        w1_lo = sb("w1_lo", [P, W1COLS], f16)
        gup_sb = sb("gup_sb", [P, EXPERTS, 2, P])
        gup_hi = sb("gup_hi", [P, EXPERTS, 2, P], f16)
        gup_lo = sb("gup_lo", [P, EXPERTS, 2, P], f16)
        down_sb = sb("down_sb", [P, EXPERTS, P])
        db_sb = sb("db_sb", [2 * EXPERTS, P])
        db_hi = sb("db_hi", [2 * EXPERTS, P], f16)
        db_lo = sb("db_lo", [2 * EXPERTS, P], f16)

        x1n = xn
        dxn = sb("dxn", [P, BT, P])
        x1T_hi = sb("x1T_hi", [P, TOKENS + KEYS], f16)
        x1T_lo = sb("x1T_lo", [P, TOKENS + KEYS], f16)
        dkT = sb("dkT", [P, CHUNK])
        dvT = sb("dvT", [P, CHUNK])
        v1T = sb("v1T", [P, CHUNK])
        qk = sb("qk", [P, 2, CHUNK])
        att = sb("att", [P, 2, CHUNK])
        adv = sb("adv", [P, 2, CHUNK])
        ctxT = sb("ctxT", [P, 2, CHUNK])
        sT = xnb[:, :, :].rearrange("p t d -> p (t d)")

        TE = [P, TILES, EXPERTS]
        logits = sb("logits", TE)
        logits2 = sb("logits2", TE)
        equal = sb("equal", TE)
        ranked = sb("ranked", TE)
        first = sb("first", TE)
        second = sb("second", TE)
        wrow = sb("wrow", TE)
        top1 = sb("top1", [P, TILES])
        top2 = sb("top2", [P, TILES])
        best = sb("best", [P, TILES])
        gap = sb("gap", [P, TILES])
        wtop1 = sb("wtop1", [P, TILES])
        wtop2 = sb("wtop2", [P, TILES])
        w16 = sb("w16", [P, TILES, 2 * EXPERTS], f16)
        wT16 = sb("wT16", [2 * EXPERTS, TOKENS], f16)

        def pair(big, k):
            return big[:, k * 2 * CT:(k + 1) * 2 * CT, :].rearrange("p (j t) d -> p j (t d)", j=2)

        g_c, g_s = pair(gate0, 0), pair(gate0, 1)
        u_b, u_c = pair(x_sb, 0), pair(x_sb, 1)
        glu, act32, actw = yT[:, 0:2, :], yT[:, 2:4, :], hT32
        o_sig = sb("o_sig", [P, CHUNK])
        o_mul = sb("o_mul", [P, CHUNK])
        prodT = sb("prodT", [P, CHUNK])
        x2 = sb("x2", [P, 2, CT, P])

        S = [ctx.enter_context(nc.psum_tensor(f"S{i}", [P, 2 * CHUNK], f32)) for i in range(2)]
        T = [ctx.enter_context(nc.psum_tensor(f"T{i}", [P, CHUNK], f32)) for i in range(2)]
        O = [ctx.enter_context(nc.psum_tensor(f"O{i}", [P, CHUNK], f32)) for i in range(2)]
        SH = [S[0][:, 0:CHUNK], S[0][:, CHUNK:2 * CHUNK], S[1][:, 0:CHUNK], S[1][:, CHUNK:2 * CHUNK]]

        x_in = [sem(f"x_in{h}") for h in range(BATCHES)]
        w0_in, vecs_in, ffn_in, l1_in = sem("w0_in"), sem("vecs_in"), sem("ffn_in"), sem("l1_in")
        out_done = [sem(f"out_done{j}") for j in range(2)]
        pool_self, dve_self = sem("pool_self"), sem("dve_self")
        consts_ready, fc_ready, xnb_ready, l1w_ready = (
            sem("consts_ready"), sem("fc_ready"), sem("xnb_ready"), sem("l1w_ready"))
        A_ready, A_hi_ready, A_lo_ready = sem("A_ready"), sem("A_hi_ready"), sem("A_lo_ready")
        rstd2_ready, xn_ready, hz_ready = sem("rstd2_ready"), sem("xn_ready"), sem("hz_ready")
        xt_ready, ht_ready = sem("xt_ready"), sem("ht_ready")
        xt_hi_ready, xt_lo_ready = sem("xt_hi_ready"), sem("xt_lo_ready")
        h32_ready, h_hi_ready, h_lo_ready = sem("h32_ready"), sem("h_hi_ready"), sem("h_lo_ready")
        fc1_done, y_ready, fc2_done, u_ready, gate0_ready = (
            sem("fc1_done"), sem("y_ready"), sem("fc2_done"), sem("u_ready"), sem("gate0_ready"))
        k_done, k_hi_ready, k_lo_ready = sem("k_done"), sem("k_hi_ready"), sem("k_lo_ready")
        v_done, v_hi_ready, v_lo_ready = sem("v_done"), sem("v_hi_ready"), sem("v_lo_ready")
        s_done, max_ready, exp_done = sem("s_done"), sem("max_ready"), sem("exp_done")
        pt_done, pt_hi_ready, pt_lo_ready = sem("pt_done"), sem("pt_hi_ready"), sem("pt_lo_ready")
        o_done, o_read = sem("o_done"), sem("o_read")
        rstd1_ready, x1n_ready, dxn_ready = sem("rstd1_ready"), sem("x1n_ready"), sem("dxn_ready")
        x1t_done, x1t_hi, x1t_lo = sem("x1t_done"), sem("x1t_hi"), sem("x1t_lo")
        router_done, gap_ready, wtop_ready = sem("router_done"), sem("gap_ready"), sem("wtop_ready")
        w16_ready, wt_done, wt_ready = sem("w16_ready"), sem("wt_done"), sem("wt_ready")
        dk_done, dv_done, v1_done, q_done = sem("dk_done"), sem("dv_done"), sem("v1_done"), sem("q_done")
        kv_ready, qk_ready, hs_done, att_ready = (
            sem("kv_ready"), sem("qk_ready"), sem("hs_done"), sem("att_ready"))
        adv_ready, ctx_ready, s1_done, s1_ready = (
            sem("adv_ready"), sem("ctx_ready"), sem("s1_done"), sem("s1_ready"))
        gate_done, up_done, wb_done, down_done = (
            sem("gate_done"), sem("up_done"), sem("wb_done"), sem("down_done"))
        gc_ready, gs_ready, ub_ready, uc_ready = (
            sem("gc_ready"), sem("gs_ready"), sem("ub_ready"), sem("uc_ready"))
        glu_ready, act_ready, actw_ready = sem("glu_ready"), sem("act_ready"), sem("actw_ready")
        osig_ready, omul_ready, prod_ready, prodt_done, x2_ready = (
            sem("osig_ready"), sem("omul_ready"), sem("prod_ready"),
            sem("prodt_done"), sem("x2_ready"))

        block = ctx.enter_context(nc.Block())

        def bc(ap, n):
            return ap.unsqueeze(2).broadcast_to([P, ap.shape[1], n])

        @block.sync
        def _(sp):
            for h in range(BATCHES):
                sp.dma_start(x_sb[:, h * BT:(h + 1) * BT, :],
                             x_rows[:, h * BT:(h + 1) * BT, :]).then_inc(x_in[h], 16)
            for dst, src in ((w1_sb[:, :], w1s), (gup_sb[:, :, :, :], gup),
                             (down_sb[:, :, :], down), (db_sb[:, :], db)):
                sp.dma_start(dst, src).then_inc(l1_in, 16)
            with sp.Fori((0) // 2, (CHUNKS) // 2) as cc:
                c = 2 * cc
                for j in range(2):
                    sp.wait_ge(x2_ready, c + j + 1)
                    sp.dma_start(out_rows[:, ds((c + j) * CT, CT), :],
                                 x2[:, j, :, :]).then_inc(out_done[j], 16)
            for j in range(2):
                sp.wait_ge(out_done[j], 16 * CHUNKS // 2)

        @block.gpsimd
        def _(pool):
            g = nc.gpsimd
            n_self = [0]

            def link(ins):
                n_self[0] += 1
                ins.then_inc(pool_self, 1)
                pool.wait_ge(pool_self, n_self[0])

            def diagonal(ap, base, pattern):
                return g.affine_select(out=ap, in_=ap, compare_op=ALU.not_equal, fill=1.0,
                                       base=base, pattern=pattern, channel_multiplier=1)

            g.memset(ident[:, :], 0.0)
            g.memset(ident16[:, :], 0.0)
            g.memset(headsum[:, :], 1.0)
            for e in range(EXPERTS):
                g.memset(rank[:, e:e + 1], float(EXPERTS - e))
            link(g.memset(sel16[:, :, :], 0.0))
            diagonal(ident[:, :], 0, [[-1, P]])
            diagonal(ident16[:, :], 0, [[-1, P]])
            link(diagonal(sel16[:, :, :], 0, [[-1, EXPERTS], [0, P]]))
            diagonal(sel16[:, :, :], -EXPERTS, [[-1, EXPERTS], [0, P]])
            hs = headsum[:, :].rearrange("p (h d) -> p h d", d=HD)
            link(g.affine_select(out=hs, in_=hs, compare_op=ALU.is_ge, fill=0.0, base=0,
                                 pattern=[[-HD, HEADS], [0, HD]], channel_multiplier=1))
            link(g.affine_select(out=hs, in_=hs, compare_op=ALU.is_ge, fill=0.0, base=HD - 1,
                                 pattern=[[HD, HEADS], [0, HD]], channel_multiplier=-1))
            g.memset(wT16[0:1, 0:1], 0.0).then_inc(consts_ready, 1)

            pool.wait_ge(ffn_in, 16 * 5)
            g.tensor_scalar(fc1_w[:, :], q1_sb[:, :], -ZERO_POINT, None, ALU.add)
            link(g.tensor_scalar(fc2_w[:, :, :], q2_sb[:, :, :], -ZERO_POINT, None, ALU.add))
            link(g.tensor_tensor(fc1_w[:, :], fc1_w[:, :], s1_sb[:, :], ALU.mult))
            g.tensor_tensor(fc2_w[:, :, :], fc2_w[:, :, :], s2_sb[:, :, :], ALU.mult)
            g.tensor_scalar(b2_sb[:, :], b2_sb[:, :], 0.5, None, ALU.mult)
            link(g.tensor_copy(fc1_hi[:, :], fc1_w[:, :]))
            g.tensor_tensor(fc1_lo[:, :], fc1_w[:, :], fc1_hi[:, :], ALU.subtract)
            pool.wait_ge(w0_in, 16)
            link(g.tensor_copy(wv_hi[:, :], w0_sb[:, WVT, :]))
            g.tensor_tensor(wv_lo[:, :], w0_sb[:, WVT, :], wv_hi[:, :],
                            ALU.subtract).then_inc(fc_ready, 1)

            with pool.Fori(0, TILES) as t:
                pool.wait_ge(xn_ready, t + 1)
                g.tensor_tensor(xnb[:, ds(t, 1), :], xn[:, ds(t, 1), :],
                                b2_sb[:, :].unsqueeze(1), ALU.add).then_inc(xnb_ready, 1)

            pool.wait_ge(l1_in, 16 * 4)
            pool.wait_ge(vecs_in, 16)
            g.tensor_copy(w1_hi[:, :], w1_sb[:, :])
            g.tensor_copy(db_hi[:, :], db_sb[:, :])
            link(g.tensor_copy(gup_hi[:, :, :, :], gup_sb[:, :, :, :]))
            g.tensor_tensor(w1_lo[:, :], w1_sb[:, :], w1_hi[:, :], ALU.subtract)
            g.tensor_tensor(db_lo[:, :], db_sb[:, :], db_hi[:, :], ALU.subtract)
            g.tensor_scalar(ub1[:, :], vecs_sb[:, UB:UB + EXPERTS], 1.0, None, ALU.add)
            g.tensor_tensor(gup_lo[:, :, :, :], gup_sb[:, :, :, :], gup_hi[:, :, :, :],
                            ALU.subtract).then_inc(l1w_ready, 1)

            pool.wait_ge(rstd1_ready, 1)
            for t in range(BT):
                g.tensor_scalar(x1n[:, t, :], x1[:, t, :], mv1[:, t, 0:1], rstd1[:, t:t + 1],
                                ALU.subtract, ALU.mult).then_inc(x1n_ready, 1)
            pool.wait_ge(x1n_ready, TILES)
            g.tensor_tensor(dxn[:, :, :], x1n[:, 0:BT, :], x1n[:, BT:TILES, :],
                            ALU.subtract).then_inc(dxn_ready, 1)

            with pool.Fori(0, 2) as j:
                for s in range(2):
                    pool.wait_ge(att_ready, 2 * j + s + 1)
                    g.tensor_tensor(adv[:, s, :], att[:, s, :], dvT[:, :],
                                    ALU.mult).then_inc(adv_ready, 1)
                    pool.wait_ge(adv_ready, 2 * j + s + 1)
                    g.tensor_tensor(ctxT[:, s, :], adv[:, s, :], v1T[:, :],
                                    ALU.add).then_inc(ctx_ready, 1)

            def product(n, e):
                pool.wait_ge(glu_ready, n + 1)
                if not (isinstance(n, int) and n < 2):
                    pool.wait_ge(actw_ready, n - 1)
                g.tensor_tensor(act32[:, e % 2, :], u_c[:, e % 2, :], glu[:, e % 2, :],
                                ALU.mult).then_inc(act_ready, 1)

            def gate_part(c):
                pool.wait_ge(osig_ready, c + 1)
                g.tensor_tensor(o_mul[:, :], o_sig[:, :], sT[:, ds(c * CHUNK, CHUNK)],
                                ALU.mult).then_inc(omul_ready, 1)

            for e in range(EXPERTS):
                product(e, e)
            with pool.Fori(1, CHUNKS) as c:
                for e in range(EXPERTS):
                    product(EXPERTS * c + e, e)
                    if e == 1:
                        gate_part(c - 1)
            gate_part(CHUNKS - 1)

        @block.scalar
        def _(act):
            a = nc.scalar
            act.dma_start(w0_sb[:, :, :], w0).then_inc(w0_in, 16)
            act.dma_start(vecs_sb[:, :], vecs).then_inc(vecs_in, 16)
            for dst, src in ((q1_sb[:, :], q1), (s1_sb[:, :], s1.partition_broadcast(P)),
                             (q2_sb[:, :, :], q2), (s2_sb[:, :, :], s2.partition_broadcast(P)),
                             (b2_sb[:, :], b2.partition_broadcast(P))):
                act.dma_start(dst, src).then_inc(ffn_in, 16)

            act.wait_ge(A_ready, 1)
            a.copy(A_hi[:, :], S[0][:, 0:P]).then_inc(A_hi_ready, 1)

            act.wait_ge(vecs_in, 16)
            for h in range(BATCHES):
                act.wait_ge(rstd2_ready, h + 1)
                with act.Fori(h * BT, (h + 1) * BT) as t:
                    act.wait_ge(xn_ready, t + 1)
                    a.activation(hz[:, ds(t, 1), :], xn[:, ds(t, 1), :], ACT.Copy,
                                 scale=rstd2[:, ds(t, 1)]).then_inc(hz_ready, 1)
                for c in range(h * 2, h * 2 + 2):
                    act.wait_ge(xt_ready, c + 1)
                    a.copy(xT_hi[:, c * CHUNK:(c + 1) * CHUNK], T[c % 2][:, :]).then_inc(xt_hi_ready, 1)
                    act.wait_ge(ht_ready, c + 1)
                    if c >= 2:
                        act.wait_ge(h_lo_ready, c - 1)
                    a.activation(hT32[:, c % 2, :], O[c % 2][:, :], ACT.Identity,
                                 bias=vecs_sb[:, BETA:BETA + 1],
                                 scale=vecs_sb[:, GAMMA:GAMMA + 1]).then_inc(h32_ready, 1)

            with act.Fori(0, CHUNKS) as c:
                for f in range(FB):
                    act.wait_ge(fc1_done, FB * c + f + 1)
                    a.activation(yT[:, f, :], SH[f], ACT.Silu,
                                 bias=vecs_sb[:, FC1B + f:FC1B + f + 1]).then_inc(y_ready, 1)
                act.wait_ge(k_done, c + 1)
                a.copy(kT_hi[:, ds(c * CHUNK, CHUNK)], T[0][:, :]).then_inc(k_hi_ready, 1)
                act.wait_ge(v_done, c + 1)
                a.copy(v_hi[:, ds(c * CT, CT), :],
                       T[1][:, :].rearrange("p (t d) -> p t d", d=P)).then_inc(v_hi_ready, 1)
                act.wait_ge(u_ready, c + 1)
                a.activation(gate0[:, ds(c * CT, CT), :],
                             u0[:, 0, :].rearrange("p (t d) -> p t d", d=P),
                             ACT.Silu).then_inc(gate0_ready, 1)

            def exp(t, j):
                act.wait_ge(max_ready, t + 1)
                a.activation(probs[:, j, :], S[j][:, :], ACT.Exp, bias=neg_max[:, ds(t, 1)],
                             accum_out=row_sum[:, ds(t, 1)]).then_inc(exp_done, 1)

            def split_hi(t, j):
                for h in range(2):
                    act.wait_ge(pt_done, 2 * t + h + 1)
                    a.copy(pT_hi[:, h * CHUNK:(h + 1) * CHUNK], T[h][:, :]).then_inc(pt_hi_ready, 1)

            exp(0, 0)
            exp(1, 1)
            for b in range(BATCHES):
                with act.Fori((b * BT) // 2, (b * BT + BT - 2) // 2) as tt:
                    t = 2 * tt
                    for j in range(2):
                        split_hi(t + j, j)
                        exp(t + j + 2, j)
                for j in range(2):
                    t = b * BT + BT - 2 + j
                    split_hi(t, j)
                    if t + 2 < TILES:
                        exp(t + 2, j)

            with act.Fori((0) // 2, (CHUNKS + 2) // 2) as cc:
                c = 2 * cc
                for j in range(2):
                    act.wait_ge(x1t_done, c + j + 1)
                    a.copy(x1T_hi[:, ds((c + j) * CHUNK, CHUNK)], T[j][:, :]).then_inc(x1t_hi, 1)

            for j in range(2):
                if j:
                    act.wait_ge(ctx_ready, 2 * j)
                act.wait_ge(dk_done, j + 1)
                a.copy(dkT[:, :], SH[0]).then_inc(kv_ready, 1)
                act.wait_ge(dv_done, j + 1)
                a.copy(dvT[:, :], SH[1]).then_inc(kv_ready, 1)
                act.wait_ge(v1_done, j + 1)
                a.activation(v1T[:, :], SH[2], ACT.Identity,
                             bias=vecs_sb[:, BV:BV + 1]).then_inc(kv_ready, 1)
                for s in range(2):
                    act.wait_ge(hs_done, 2 * j + s + 1)
                    a.activation(att[:, s, :], (SH[3], O[1][:, :])[s], ACT.Sigmoid,
                                 scale=HEAD_SCALE).then_inc(att_ready, 1)
                if j == 0:
                    act.wait_ge(gap_ready, 1)
                    a.activation(wtop1[:, :], gap[:, :], ACT.Sigmoid)
                    a.activation(wtop2[:, :], gap[:, :], ACT.Sigmoid, scale=-1.0).then_inc(wtop_ready, 1)
                for s in range(2):
                    act.wait_ge(s1_done, 2 * j + s + 1)
                    a.activation(sT[:, (j + 2 * s) * CHUNK:(j + 2 * s + 1) * CHUNK], (T[0], T[1])[s][:, :],
                                 ACT.Identity, bias=vecs_sb[:, BO:BO + 1]).then_inc(s1_ready, 1)

            act.wait_ge(l1w_ready, 1)

            def expert(n, e):
                late = not (isinstance(n, int) and n < 2)
                act.wait_ge(up_done, n + 1)
                if late:
                    act.wait_ge(uc_ready, n - 1)
                a.activation(u_b[:, e % 2, :], SH[2 + e % 2], ACT.Identity,
                             bias=ub1[:, e:e + 1]).then_inc(ub_ready, 1)
                act.wait_ge(gc_ready, n + 1)
                if late:
                    act.wait_ge(glu_ready, n - 1)
                a.activation(g_s[:, e % 2, :], g_c[:, e % 2, :], ACT.Sigmoid,
                             scale=ALPHA).then_inc(gs_ready, 1)

            def finish(c):
                act.wait_ge(down_done, EXPERTS * (c + 1))
                act.wait_ge(omul_ready, c)
                a.activation(o_sig[:, :], O[0][:, :], ACT.Sigmoid).then_inc(osig_ready, 1)

            for e in range(EXPERTS):
                expert(e, e)
            with act.Fori(1, CHUNKS) as c:
                for e in range(EXPERTS):
                    expert(EXPERTS * c + e, e)
                    if e == 1:
                        finish(c - 1)
            finish(CHUNKS - 1)

        @block.vector
        def _(dve):
            v = nc.vector
            n_self = [0]

            def link(ins):
                n_self[0] += 1
                ins.then_inc(dve_self, 1)
                dve.wait_ge(dve_self, n_self[0])

            def rsqrt(y, a_, n0, n1):
                r = slice(n0, n1)
                v.tensor_scalar(half_a[:, r], a_, -0.5, None, ALU.mult)
                link(v.tensor_scalar(seed[:, r], a_.bitcast(i32), 1, None, ALU.logical_shift_right))
                link(v.tensor_scalar(seed[:, r], seed[:, r], -1.0, RSQRT_MAGIC, ALU.mult, ALU.add))
                src = seed[:, r].bitcast(f32)
                for k in range(4):
                    link(v.tensor_tensor(newt[:, r], src, src, ALU.mult))
                    link(v.tensor_tensor(newt2[:, r], newt[:, r], half_a[:, r], ALU.mult))
                    link(v.scalar_tensor_tensor(y[:, r], newt2[:, r], 1.5, src, ALU.add, ALU.mult))
                    src = y[:, r]

            dve.wait_ge(A_hi_ready, 1)
            v.tensor_tensor(A_lo[:, :], S[0][:, 0:P], A_hi[:, :], ALU.subtract).then_inc(A_lo_ready, 1)

            for h in range(BATCHES):
                r = slice(h * BT, (h + 1) * BT)
                dve.wait_ge(x_in[h], 16)
                for t in range(h * BT, (h + 1) * BT):
                    ins = v.bn_stats(stats[:, t, :], x_sb[:, t, :])
                link(ins)
                for t in range(h * BT, (h + 1) * BT):
                    ins = v.bn_aggr(mv[:, t, :], stats[:, t, :])
                link(ins)
                link(v.tensor_scalar(var_e[:, r], mv[:, r, 1], EPS, None, ALU.add))
                rsqrt(rstd, var_e[:, r], h * BT, (h + 1) * BT)
                for t in range(h * BT, (h + 1) * BT):
                    v.tensor_scalar(xn[:, t, :], x_sb[:, t, :], mv[:, t, 0:1], rstd[:, t:t + 1],
                                    ALU.subtract, ALU.mult).then_inc(xn_ready, 1)
                link(v.tensor_tensor(var_e[:, r], mv[:, r, 1], rstd[:, r], ALU.mult))
                link(v.tensor_tensor(var_e[:, r], var_e[:, r], rstd[:, r], ALU.mult))
                link(v.tensor_scalar(var_e[:, r], var_e[:, r], EPS, None, ALU.add))
                rsqrt(rstd2, var_e[:, r], h * BT, (h + 1) * BT)
                v.tensor_copy(newt[:, r], rstd2[:, r]).then_inc(rstd2_ready, 1)

            for c in range(CHUNKS):
                r = slice(c * CHUNK, (c + 1) * CHUNK)
                dve.wait_ge(xt_hi_ready, c + 1)
                v.tensor_tensor(xT_lo[:, r], T[c % 2][:, :], xT_hi[:, r],
                                ALU.subtract).then_inc(xt_lo_ready, 1)
                dve.wait_ge(h32_ready, c + 1)
                v.tensor_copy(hT_hi[:, r], hT32[:, c % 2, :]).then_inc(h_hi_ready, 1)
                dve.wait_ge(h_hi_ready, c + 1)
                v.tensor_tensor(hT_lo[:, r], hT32[:, c % 2, :], hT_hi[:, r],
                                ALU.subtract).then_inc(h_lo_ready, 1)

            with dve.Fori(0, CHUNKS) as c:
                dve.wait_ge(k_hi_ready, c + 1)
                v.tensor_tensor(kT_lo[:, ds(c * CHUNK, CHUNK)], T[0][:, :],
                                kT_hi[:, ds(c * CHUNK, CHUNK)], ALU.subtract).then_inc(k_lo_ready, 1)
                dve.wait_ge(v_hi_ready, c + 1)
                v.tensor_tensor(v_lo[:, ds(c * CT, CT), :], T[1][:, :].rearrange("p (t d) -> p t d", d=P),
                                v_hi[:, ds(c * CT, CT), :], ALU.subtract).then_inc(v_lo_ready, 1)
                dve.wait_ge(fc2_done, c + 1)
                dve.wait_ge(xnb_ready, CT * c + CT)
                dve.wait_ge(gate0_ready, c)
                v.scalar_tensor_tensor(u0[:, 0, :].rearrange("p (t d) -> p t d", d=P),
                                       O[0][:, :].rearrange("p (t d) -> p t d", d=P), 0.5,
                                       xnb[:, ds(c * CT, CT), :], ALU.mult, ALU.add).then_inc(u_ready, 1)

            def row_max(t, j):
                dve.wait_ge(s_done, t + 1)
                v.tensor_reduce(neg_max[:, ds(t, 1)], S[j][:, :], AX.X, ALU.max,
                                negate=True).then_inc(max_ready, 1)

            def split_lo(t, j):
                for h in range(2):
                    r = slice(h * CHUNK, (h + 1) * CHUNK)
                    dve.wait_ge(pt_hi_ready, 2 * t + h + 1)
                    v.tensor_tensor(pT_lo[:, r], T[h][:, :], pT_hi[:, r],
                                    ALU.subtract).then_inc(pt_lo_ready, 1)

            LPT = 3

            def rows(t, j, base):
                def step(k, ins):
                    ins.then_inc(dve_self, 1)
                    dve.wait_ge(dve_self, base + k)

                step(1, v.reciprocal(row_inv[:, ds(t, 1)], row_sum[:, ds(t, 1)]))
                dve.wait_ge(o_done, t + 1)
                ins = v.scalar_tensor_tensor(sg0[:, j:j + 1, :], O[j][:, 0:P].unsqueeze(1),
                                             row_inv[:, ds(t, 1)], gate0[:, ds(t, 1), :],
                                             ALU.mult, ALU.mult)
                ins.then_inc(o_read, 1)
                dve.wait_ge(o_read, t + 1)
                step(2, v.scalar_tensor_tensor(x1[:, ds(t, 1), :], sg0[:, j:j + 1, :], NORM_FACT,
                                               x_sb[:, ds(t, 1), :], ALU.mult, ALU.add))
                step(3, v.bn_stats(stats1[:, ds(t, 1), :].rearrange("p a b -> p (a b)"),
                                   x1[:, ds(t, 1), :].rearrange("p a b -> p (a b)")))

            dve.wait_ge(gate0_ready, CHUNKS)
            row_max(0, 0)
            row_max(1, 1)
            for b in range(BATCHES):
                base = n_self[0]
                with dve.Fori((b * BT) // 2, (b * BT + BT - 2) // 2) as tt:
                    t = 2 * tt
                    for j in range(2):
                        split_lo(t + j, j)
                        row_max(t + j + 2, j)
                        rows(t + j, j, base - LPT * b * BT + LPT * (t + j))
                n_self[0] += LPT * (BT - 2)
                for j in range(2):
                    t = b * BT + BT - 2 + j
                    split_lo(t, j)
                    if t + 2 < TILES:
                        row_max(t + 2, j)
                    rows(t, j, n_self[0])
                    n_self[0] += LPT
                r = slice(b * BT, (b + 1) * BT)
                for t in range(b * BT, (b + 1) * BT):
                    ins = v.bn_aggr(mv1[:, t, :], stats1[:, t, :])
                link(ins)
                link(v.tensor_scalar(var_e[:, r], mv1[:, r, 1], EPS, None, ALU.add))
                rsqrt(rstd1, var_e[:, r], b * BT, (b + 1) * BT)
                if b == 0:
                    v.tensor_copy(newt[:, r], rstd1[:, r]).then_inc(rstd1_ready, 1)
            dve.wait_ge(x1n_ready, BT)
            for t in range(BT, TILES):
                v.tensor_scalar(x1n[:, t, :], x1[:, t, :], mv1[:, t, 0:1], rstd1[:, t:t + 1],
                                ALU.subtract, ALU.mult).then_inc(x1n_ready, 1)

            with dve.Fori((0) // 2, (CHUNKS + 2) // 2) as cc:
                c = 2 * cc
                for j in range(2):
                    dve.wait_ge(x1t_hi, c + j + 1)
                    v.tensor_tensor(x1T_lo[:, ds((c + j) * CHUNK, CHUNK)], T[j][:, :],
                                    x1T_hi[:, ds((c + j) * CHUNK, CHUNK)],
                                    ALU.subtract).then_inc(x1t_lo, 1)

            def scores(j):
                dve.wait_ge(kv_ready, 3 * j + 1)
                if j:
                    dve.wait_ge(hs_done, 2 * j)
                for s in range(2):
                    dve.wait_ge(q_done, 2 * j + s + 1)
                    v.scalar_tensor_tensor(qk[:, s, :], T[s][:, :], vecs_sb[:, BQ:BQ + 1], dkT[:, :],
                                           ALU.add, ALU.mult).then_inc(qk_ready, 1)

            scores(0)
            lg, l2 = logits[:, :, :], logits2[:, :, :]
            dve.wait_ge(router_done, 1)
            link(v.tensor_copy(lg, O[0][:, 0:TILES * EXPERTS].rearrange("p (t e) -> p t e", e=EXPERTS)))
            rank_b = rank[:, :].unsqueeze(1).broadcast_to(TE)
            for src, top, one_hot in ((lg, top1, first), (l2, top2, second)):
                link(v.tensor_reduce(top[:, :], src, AX.X, ALU.max))
                link(v.tensor_tensor(equal[:, :, :], src, bc(top[:, :], EXPERTS), ALU.is_equal))
                link(v.tensor_tensor(ranked[:, :, :], equal[:, :, :], rank_b, ALU.mult))
                link(v.tensor_reduce(best[:, :], ranked[:, :, :], AX.X, ALU.max))
                link(v.tensor_tensor(one_hot[:, :, :], ranked[:, :, :], bc(best[:, :], EXPERTS),
                                     ALU.is_equal))
                if one_hot is first:
                    link(v.scalar_tensor_tensor(l2, first[:, :, :], LOWEST, lg, ALU.mult, ALU.add))
            v.tensor_tensor(gap[:, :], top1[:, :], top2[:, :], ALU.subtract).then_inc(gap_ready, 1)
            dve.wait_ge(wtop_ready, 1)
            link(v.tensor_tensor(first[:, :, :], first[:, :, :], bc(wtop1[:, :], EXPERTS), ALU.mult))
            link(v.tensor_tensor(second[:, :, :], second[:, :, :], bc(wtop2[:, :], EXPERTS), ALU.mult))
            link(v.tensor_tensor(wrow[:, :, :], first[:, :, :], second[:, :, :], ALU.add))
            link(v.tensor_copy(w16[:, :, 0:EXPERTS], wrow[:, :, :]))
            v.tensor_tensor(w16[:, :, EXPERTS:2 * EXPERTS], wrow[:, :, :], w16[:, :, 0:EXPERTS],
                            ALU.subtract).then_inc(w16_ready, 1)
            scores(1)
            for h in range(BATCHES):
                dve.wait_ge(wt_done, h + 1)
                v.tensor_copy(wT16[:, h * KEYS:(h + 1) * KEYS],
                              SH[h][0:2 * EXPERTS, :].bitcast(f16)).then_inc(wt_ready, 1)

            def clip_gate(n, e):
                dve.wait_ge(gate_done, n + 1)
                v.tensor_scalar(g_c[:, e % 2, :], SH[e % 2], vecs_sb[:, GB + e:GB + e + 1], LIMIT,
                                ALU.add, ALU.min).then_inc(gc_ready, 1)

            def clip_up(n, e):
                dve.wait_ge(ub_ready, n + 1)
                v.tensor_scalar(u_c[:, e % 2, :], u_b[:, e % 2, :], LIMIT + 1.0, 1.0 - LIMIT,
                                ALU.min, ALU.max).then_inc(uc_ready, 1)

            def gated(n, e):
                dve.wait_ge(gs_ready, n + 1)
                v.tensor_tensor(glu[:, e % 2, :], g_c[:, e % 2, :], g_s[:, e % 2, :],
                                ALU.mult).then_inc(glu_ready, 1)

            def weigh(n, e):
                dve.wait_ge(act_ready, n + 1)
                dve.wait_ge(wb_done, n + 1)
                if not (isinstance(n, int) and n < 2):
                    dve.wait_ge(down_done, n - 1)
                v.tensor_tensor(actw[:, e % 2, :], act32[:, e % 2, :], T[e % 2][:, :],
                                ALU.mult).then_inc(actw_ready, 1)

            def step(n, e):
                clip_gate(n, e)
                clip_up(n, e)
                gated(n, e)
                if not (isinstance(n, int) and n < 1):
                    weigh(n - 1, (e - 1) % EXPERTS)

            def gate_product(c):
                dve.wait_ge(omul_ready, c + 1)
                if not (isinstance(c, int) and c < 1):
                    dve.wait_ge(prodt_done, c)
                v.tensor_tensor(prodT[:, :], O[0][:, :], o_mul[:, :], ALU.mult).then_inc(prod_ready, 1)

            def last_rows(c, slot):
                dve.wait_ge(prodt_done, c + 1)
                if c >= 2:
                    dve.wait_ge(out_done[slot], 16 * (c // 2))
                v.tensor_tensor(x2[:, slot, :, :], O[1][:, :].rearrange("p (t d) -> p t d", d=P),
                                x1[:, ds(c * CT, CT), :], ALU.add).then_inc(x2_ready, 1)

            for e in range(EXPERTS):
                step(e, e)
            for c in range(1, CHUNKS):
                for e in range(EXPERTS):
                    if e == 2:
                        gate_product(c - 1)
                    if e == 4:
                        last_rows(c - 1, (c - 1) % 2)
                    step(EXPERTS * c + e, e)
            weigh(EXPERTS * CHUNKS - 1, EXPERTS - 1)
            gate_product(CHUNKS - 1)
            last_rows(CHUNKS - 1, (CHUNKS - 1) % 2)

        @block.tensor
        def _(pe):
            mm = nc.tensor.matmul

            def three(o, l_hi, l_lo, r_hi, r_lo):
                mm(o, l_hi, r_hi, start=True, stop=False)
                mm(o, l_hi, r_lo, start=False, stop=False)
                return mm(o, l_lo, r_hi, start=False, stop=True)

            pe.wait_ge(w0_in, 16)
            mm(S[0][:, 0:P], w0_sb[:, WK, :], w0_sb[:, WQ, :], start=True, stop=True).then_inc(A_ready, 1)

            pe.wait_ge(consts_ready, 1)
            for c in range(CHUNKS):
                for src, rows_ready, bank, done, free in (
                        (xn, xn_ready, T[c % 2], xt_ready, xt_lo_ready),
                        (hz, hz_ready, O[c % 2], ht_ready, h32_ready)):
                    pe.wait_ge(rows_ready, CT * (c + 1))
                    if c >= 2:
                        pe.wait_ge(free, c - 1)
                    for k in range(CT):
                        ins = nc.tensor.transpose(bank[:, k * P:(k + 1) * P], src[:, CT * c + k, :],
                                                  ident[:, :])
                    ins.then_inc(done, 1)

            pe.wait_ge(fc_ready, 1)
            pe.wait_ge(A_lo_ready, 1)
            pe.wait_ge(xt_lo_ready, CHUNKS)
            pe.wait_ge(h_lo_ready, CHUNKS)
            with pe.Fori(0, CHUNKS) as c:
                cols = ds(c * CHUNK, CHUNK)
                for f in range(FB):
                    w = slice(f * P, (f + 1) * P)
                    pe.wait_ge(y_ready, FB * c)
                    three(SH[f], fc1_hi[:, w], fc1_lo[:, w], hT_hi[:, cols],
                          hT_lo[:, cols]).then_inc(fc1_done, 1)
                pe.wait_ge(k_lo_ready, c)
                three(T[0][:, :], A_hi[:, :], A_lo[:, :], xT_hi[:, cols], xT_lo[:, cols]).then_inc(k_done, 1)
                pe.wait_ge(v_lo_ready, c)
                for k in range(CT):
                    tok = ds(c * CHUNK + k * P, P)
                    ins = three(T[1][:, k * P:(k + 1) * P], xT_hi[:, tok], xT_lo[:, tok],
                                wv_hi[:, :], wv_lo[:, :])
                ins.then_inc(v_done, 1)
                pe.wait_ge(u_ready, c)
                for k in range(CT):
                    for f in range(FB):
                        if k == 0:
                            pe.wait_ge(y_ready, FB * c + f + 1)
                        ins = mm(O[0][:, k * P:(k + 1) * P], yT[:, f, k * P:(k + 1) * P], fc2_w[:, f, :],
                                 start=(f == 0), stop=(f == FB - 1))
                ins.then_inc(fc2_done, 1)

            def logit(t, j, b):
                if not (isinstance(t, int) and t < 2):
                    pe.wait_ge(exp_done, t - 1)
                q = ds(t * P, P)
                for h in range(2):
                    keys = slice(b * KEYS + h * CHUNK, b * KEYS + (h + 1) * CHUNK)
                    ins = three(S[j][:, h * CHUNK:(h + 1) * CHUNK], xT_hi[:, q], xT_lo[:, q],
                                kT_hi[:, keys], kT_lo[:, keys])
                ins.then_inc(s_done, 1)

            def turn(t, j):
                pe.wait_ge(exp_done, t + 1)
                for h in range(2):
                    if not (isinstance(t, int) and t < 1):
                        pe.wait_ge(pt_lo_ready, 2 * t - 1 + h)
                    for k in range(CT):
                        at = h * CHUNK + k * P
                        ins = nc.tensor.transpose(T[h][:, k * P:(k + 1) * P], probs[:, j, at:at + P],
                                                  ident[:, :])
                    ins.then_inc(pt_done, 1)

            def weighted(t, j, b):
                if not (isinstance(t, int) and t < 2):
                    pe.wait_ge(o_read, t - 1)
                for m in range(BT):
                    if m % CT == 0:
                        pe.wait_ge(pt_lo_ready, 2 * t + m // CT + 1)
                    at, vt = slice(m * P, (m + 1) * P), b * BT + m
                    for n, (l, r) in enumerate(((pT_hi, v_hi), (pT_hi, v_lo), (pT_lo, v_hi))):
                        ins = mm(O[j][:, 0:P], l[:, at], r[:, vt, :], start=(m == 0 and n == 0),
                                 stop=(m == BT - 1 and n == 2))
                ins.then_inc(o_done, 1)

            pe.wait_ge(y_ready, FB * CHUNKS)
            pe.wait_ge(k_lo_ready, CHUNKS)
            pe.wait_ge(v_lo_ready, CHUNKS)
            logit(0, 0, 0)
            logit(1, 1, 0)
            pe.wait_ge(u_ready, CHUNKS)
            for j in range(2):
                turn(j, j)
                logit(j + 2, j, 0)
                weighted(j, j, 0)
            for b in range(BATCHES):
                with pe.Fori((b * BT) // 2 + (b == 0), (b * BT + BT - 2) // 2) as tt:
                    t = 2 * tt
                    for j in range(2):
                        turn(t + j, j)
                        logit(t + j + 2, j, b)
                        weighted(t + j, j, b)
                for j in range(2):
                    t = b * BT + BT - 2 + j
                    turn(t, j)
                    if t + 2 < TILES:
                        logit(t + 2, j, b + 1)
                    weighted(t, j, b)

            pe.wait_ge(l1w_ready, 1)
            for c in range(CHUNKS + 2):
                if c < CHUNKS:
                    pe.wait_ge(x1n_ready, CT * (c + 1))
                else:
                    pe.wait_ge(dxn_ready, 1)
                pe.wait_ge(*((x1t_lo, c - 1) if c >= 2 else (pt_lo_ready, 2 * TILES)))
                for k in range(CT):
                    src = x1n[:, CT * c + k, :] if c < CHUNKS else dxn[:, CT * (c - CHUNKS) + k, :]
                    ins = nc.tensor.transpose(T[c % 2][:, k * P:(k + 1) * P], src, ident[:, :])
                ins.then_inc(x1t_done, 1)

            wr = slice(OUT * P + P, OUT * P + P + EXPERTS)
            pe.wait_ge(o_read, TILES)
            with pe.Fori(0, CHUNKS) as c:
                pe.wait_ge(x1t_lo, c + 1)
                for k in range(CT):
                    tok = ds(c * CHUNK + k * P, P)
                    three(O[0][:, ds((CT * c + k) * EXPERTS, EXPERTS)], x1T_hi[:, tok], x1T_lo[:, tok],
                          w1_hi[:, wr], w1_lo[:, wr])
            last = slice(TOKENS - P, TOKENS)
            three(O[0][:, (TILES - 1) * EXPERTS:TILES * EXPERTS], x1T_hi[:, last], x1T_lo[:, last],
                  w1_hi[:, wr], w1_lo[:, wr]).then_inc(router_done, 1)

            def proj(bank, i, c):
                w, cols = slice(i * P, (i + 1) * P), slice(c * CHUNK, (c + 1) * CHUNK)
                return three(bank, w1_hi[:, w], w1_lo[:, w], x1T_hi[:, cols], x1T_lo[:, cols])

            pe.wait_ge(exp_done, TILES)
            pe.wait_ge(x1t_lo, CHUNKS + 2)
            for j in range(2):
                if j:
                    pe.wait_ge(kv_ready, 3 * j)
                proj(SH[0], IK, CHUNKS + j).then_inc(dk_done, 1)
                proj(SH[1], IV, CHUNKS + j).then_inc(dv_done, 1)
                proj(SH[2], IV, 2 + j).then_inc(v1_done, 1)
                if j:
                    pe.wait_ge(s1_ready, 2 * j)
                for s in range(2):
                    proj(T[s][:, :], IQ, j + 2 * s).then_inc(q_done, 1)
                for s in range(2):
                    pe.wait_ge(qk_ready, 2 * j + s + 1)
                    mm((SH[3], O[1][:, :])[s], headsum[:, :], qk[:, s, :], start=True,
                       stop=True).then_inc(hs_done, 1)
                for s in range(2):
                    pe.wait_ge(ctx_ready, 2 * j + s + 1)
                    mm(T[s][:, :], w1_sb[:, OUT * P:OUT * P + P], ctxT[:, s, :], start=True,
                       stop=True).then_inc(s1_done, 1)

            pe.wait_ge(w16_ready, 1)
            pe.wait_ge(kv_ready, 6)
            for h in range(BATCHES):
                for k in range(BT):
                    ins = nc.tensor.transpose(SH[h][0:2 * EXPERTS, :].bitcast(f16)[:, k * P:(k + 1) * P],
                                              w16[:, h * BT + k, :], ident16[:, :])
                ins.then_inc(wt_done, 1)
            pe.wait_ge(wt_ready, BATCHES)
            pe.wait_ge(s1_ready, 4)

            def up_side(n, e, c):
                cols = ds(c * CHUNK, CHUNK)
                late = not (isinstance(n, int) and n < 2)
                if late:
                    pe.wait_ge(gc_ready, n - 1)
                three(SH[e % 2], gup_hi[:, e, 0, :], gup_lo[:, e, 0, :], x1T_hi[:, cols],
                      x1T_lo[:, cols]).then_inc(gate_done, 1)
                if late:
                    pe.wait_ge(ub_ready, n - 1)
                three(SH[2 + e % 2], gup_hi[:, e, 1, :], gup_lo[:, e, 1, :], x1T_hi[:, cols],
                      x1T_lo[:, cols]).then_inc(up_done, 1)
                if late:
                    pe.wait_ge(actw_ready, n - 1)
                mm(T[e % 2][:, :], sel16[:, e, :], wT16[:, cols], start=True, stop=True).then_inc(wb_done, 1)

            def down_side(n, e, c):
                if e == 0:
                    if not (isinstance(c, int) and c < 1):
                        pe.wait_ge(prod_ready, c)
                    mm(O[0][:, :], db_hi[:, :], wT16[:, ds(c * CHUNK, CHUNK)], start=True, stop=False)
                    mm(O[0][:, :], db_lo[:, :], wT16[:, ds(c * CHUNK, CHUNK)], start=False, stop=False)
                pe.wait_ge(actw_ready, n + 1)
                ins = mm(O[0][:, :], down_sb[:, e, :], actw[:, e % 2, :], start=False,
                         stop=(e == EXPERTS - 1))
                ins.then_inc(down_done, 1)

            def turn_back(c):
                pe.wait_ge(prod_ready, c + 1)
                if not (isinstance(c, int) and c < 1):
                    pe.wait_ge(x2_ready, c)
                for k in range(CT):
                    ins = nc.tensor.transpose(O[1][:, k * P:(k + 1) * P], prodT[:, k * P:(k + 1) * P],
                                              ident[:, :])
                ins.then_inc(prodt_done, 1)

            LAG = 2
            for c in range(CHUNKS):
                for e in range(EXPERTS):
                    n = EXPERTS * c + e
                    up_side(n, e, c)
                    if n >= LAG:
                        down_side(n - LAG, (e - LAG) % EXPERTS, c if e >= LAG else c - 1)
                    if e == 3 and c:
                        turn_back(c - 1)
            for e in range(EXPERTS - LAG, EXPERTS):
                down_side(EXPERTS * (CHUNKS - 1) + e, e, CHUNKS - 1)
            turn_back(CHUNKS - 1)


def kernel(**inputs):
    import numpy as np
    import concourse.bacc as bacc
    from concourse.bass_utils import run_bass_kernel_spmd

    a = {k: np.asarray(v) for k, v in inputs.items()}
    in_w = a["L1_attn_in_proj_weight"].reshape(HEADS, 3, HD, P).transpose(1, 0, 2, 3).reshape(3, P, P)
    in_b = a["L1_attn_in_proj_bias"].reshape(HEADS, 3, HD).transpose(1, 0, 2).reshape(3, P)
    gup = a["L1_ffn_gate_up_proj"].reshape(EXPERTS, P, P, 2).transpose(1, 0, 3, 2)
    gub = a["L1_ffn_gate_up_proj_bias"].reshape(EXPERTS, P, 2)
    arrays = {
        "x": a["L0_attn_x"].reshape(TOKENS, P),
        "w0": np.stack([a["L0_attn_Wq"], a["L0_attn_Wk"], a["L0_attn_Wv"].T], axis=1),
        "w1s": np.concatenate([in_w[0].T, in_w[1].T, in_w[2].T, a["L1_attn_out_proj_weight"].T,
                               a["L1_ffn_router_weight"]], axis=1),
        "vecs": np.stack([a["L0_ffn_ln_gamma"], a["L0_ffn_ln_beta"],
                          *a["L0_ffn_fc1_bias"].reshape(FB, P), in_b[0], in_b[2],
                          a["L1_attn_out_proj_bias"], *gub[:, :, 0], *gub[:, :, 1]], axis=1),
        "q1": a["L0_ffn_fc1_q"],
        "q2": a["L0_ffn_fc2_q"].reshape(FB, P, P).transpose(1, 0, 2),
        "s1": a["L0_ffn_fc1_scales"].reshape(FFN),
        "s2": a["L0_ffn_fc2_scales"],
        "b2": a["L0_ffn_fc2_bias"],
        "gup": gup,
        "down": a["L1_ffn_down_proj"].transpose(1, 0, 2),
        "db": np.concatenate([a["L1_ffn_down_proj_bias"]] * 2, axis=0),
    }
    nc = bacc.Bacc("TRN2", target_bir_lowering=False, num_devices=1)
    arrays = {k: np.ascontiguousarray(v) for k, v in arrays.items()}
    args = [nc.dram_tensor(k, v.shape, mybir.dt.from_np(v.dtype), kind="ExternalInput").ap()
            for k, v in arrays.items()]
    out = nc.dram_tensor("out", (TOKENS, P), mybir.dt.float32, kind="ExternalOutput").ap()
    build(nc, *args, out)
    r = run_bass_kernel_spmd(nc, [arrays], core_ids=[0])
    return r.results[0]["out"].reshape(BATCHES, KEYS, P)
```

```python
from contextlib import ExitStack

import concourse.bass as bass
from concourse import mybir

P = 128
TOKENS = 2048
TILES = TOKENS // P
BATCHES = 2
BT = TILES // BATCHES
KEYS = TOKENS // BATCHES
CHUNK = 512
CHUNKS = TOKENS // CHUNK
CT = CHUNK // P
FFN = 512
FB = FFN // P
EXPERTS = 8
HEADS = 16
HD = P // HEADS
EPS = 1e-5
NORM_FACT = float(P) ** -0.5
HEAD_SCALE = float(HD) ** -0.5
ZERO_POINT = 128.0
ALPHA, LIMIT = 1.702, 7.0
RSQRT_MAGIC = float(0x5F3759DF)
LOWEST = -3.0e38

GAMMA, BETA, FC1B, BQ, BV, BO, GB = 0, 1, 2, 6, 7, 8, 9
UB = GB + EXPERTS
VECS = UB + EXPERTS
WQ, WK, WVT = 0, 1, 2
IQ, IK, IV, OUT = 0, 1, 2, 3
F_ORDER = (1, 2, 3, 0)


def build(nc, x, w0, w1s, vecs, q1, q2, s1, s2, b2, gup, down, db, out):
    f32, f16, i32 = mybir.dt.float32, mybir.dt.float16, mybir.dt.int32
    ALU = mybir.AluOpType
    ACT = mybir.ActivationFunctionType
    AX = mybir.AxisListType
    ds = bass.ds

    x_rows = x.rearrange("(t p) d -> p t d", p=P)
    out_rows = out.rearrange("(t p) d -> p t d", p=P)

    ctx = ExitStack()
    with ctx:
        def sb(name, shape, dt=f32):
            return ctx.enter_context(nc.sbuf_tensor(name, shape, dt))

        def sem(name):
            return ctx.enter_context(nc.semaphore(name))

        ident = sb("ident", [P, P])
        ident16 = sb("ident16", [P, P], f16)
        headsum = sb("headsum", [P, P])
        sel16 = sb("sel16", [2 * EXPERTS, EXPERTS, P], f16)
        rank = sb("rank", [P, EXPERTS])
        scratch = sb("scratch", [P, 1])
        scratch_dve = sb("scratch_dve", [P, 3])

        x_sb = sb("x_sb", [P, TILES, P])
        xn = sb("xn", [P, TILES, P])
        hz = sb("hz", [P, TILES, P])
        xnb = sb("xnb", [P, TILES, P])
        gate0 = sb("gate0", [P, TILES, P])
        xT_hi = sb("xT_hi", [P, TOKENS], f16)
        xT_lo = sb("xT_lo", [P, TOKENS], f16)
        hT32 = sb("hT32", [P, 2, CHUNK])
        hT_hi = sb("hT_hi", [P, TOKENS], f16)
        hT_lo = sb("hT_lo", [P, TOKENS], f16)
        kT_hi = sb("kT_hi", [P, TOKENS], f16)
        kT_lo = sb("kT_lo", [P, TOKENS], f16)
        v_hi = sb("v_hi", [P, TILES, P], f16)
        v_lo = sb("v_lo", [P, TILES, P], f16)
        yT = sb("yT", [P, FB, CHUNK])
        u0 = sb("u0", [P, CHUNK])
        probs = sb("probs", [P, 2, KEYS])
        pT_hi = sb("pT_hi", [P, 2, KEYS], f16)
        pT_lo = sb("pT_lo", [P, 2, KEYS], f16)
        sg0 = sb("sg0", [P, 2, P])
        x1 = hz

        stats = sb("stats", [P, TILES, 6])
        mv = sb("mv", [P, TILES, 2])
        stats1 = sb("stats1", [P, TILES, 6])
        mv1 = sb("mv1", [P, TILES, 2])
        rs_arg = sb("rs_arg", [P, 2, TILES])
        rs = sb("rs", [P, 2, TILES])
        rs1_arg = sb("rs1_arg", [P, TILES])
        rs1 = sb("rs1", [P, TILES])
        hz_bias = sb("hz_bias", [P, TILES])
        half_a = sb("half_a", [P, 2 * TILES])
        seed = sb("seed", [P, 2 * TILES], i32)
        newt = sb("newt", [P, 2 * TILES])
        newt2 = sb("newt2", [P, 2 * TILES])
        neg_max = sb("neg_max", [P, TILES])
        row_sum = sb("row_sum", [P, TILES])
        row_inv = sb("row_inv", [P, TILES])

        w0_sb = sb("w0_sb", [P, 3, P])
        A_hi = sb("A_hi", [P, P], f16)
        A_lo = sb("A_lo", [P, P], f16)
        wv_hi = sb("wv_hi", [P, P], f16)
        wv_lo = sb("wv_lo", [P, P], f16)
        vecs_sb = sb("vecs_sb", [P, VECS])
        ub1 = sb("ub1", [P, EXPERTS])
        bo_half = sb("bo_half", [P, 1])
        q1_sb = sb("q1_sb", [P, FFN], i32)
        q2_sb = sb("q2_sb", [P, FB, P], i32)
        s1_sb = sb("s1_sb", [P, FFN])
        s2_sb = sb("s2_sb", [P, FB, P])
        b2_sb = sb("b2_sb", [P, P])
        fc1_w = sb("fc1_w", [P, FFN])
        fc1_hi = sb("fc1_hi", [P, FFN], f16)
        fc1_lo = sb("fc1_lo", [P, FFN], f16)
        fc2_w = sb("fc2_w", [P, FB, P])

        W1COLS = 4 * P + EXPERTS
        w1_sb = sb("w1_sb", [P, W1COLS])
        w1_hi = sb("w1_hi", [P, W1COLS], f16)
        w1_lo = sb("w1_lo", [P, W1COLS], f16)
        gup_sb = sb("gup_sb", [P, EXPERTS, 2, P])
        gup_hi = sb("gup_hi", [P, EXPERTS, 2, P], f16)
        gup_lo = sb("gup_lo", [P, EXPERTS, 2, P], f16)
        down_sb = sb("down_sb", [P, EXPERTS, P])
        db_sb = sb("db_sb", [2 * EXPERTS, P])
        db_hi = sb("db_hi", [2 * EXPERTS, P], f16)
        db_lo = sb("db_lo", [2 * EXPERTS, P], f16)

        x1n = xn
        dxn = sb("dxn", [P, BT, P])
        x1T_hi = sb("x1T_hi", [P, TOKENS + KEYS], f16)
        x1T_lo = sb("x1T_lo", [P, TOKENS + KEYS], f16)
        sT = xnb[:, :, :].rearrange("p t d -> p (t d)")

        dkT, dvT = (probs[:, k, :].rearrange("p (j n) -> p j n", j=2) for k in range(2))
        v1T = hT_hi[:, :].bitcast(f32).rearrange("p (j n) -> p j n", j=2)

        def quad(*halves):
            return [h.bitcast(f32).rearrange("p (s n) -> p s n", s=2) for h in halves]

        qk = quad(kT_hi[:, :], kT_lo[:, :])
        th = quad(*(v[:, :, :].rearrange("p t d -> p (t d)") for v in (v_hi, v_lo)))
        adv = quad(*(v[:, :, :].rearrange("p t d -> p (t d)") for v in (pT_hi, pT_lo)))
        ctxT = quad(xT_hi[:, :], xT_lo[:, :])

        BE = [P, BT, EXPERTS]
        logits, logits2, equal, ranked, first, second, wrow = (
            sb(name, BE) for name in ("logits", "logits2", "equal", "ranked", "first", "second", "wrow"))
        top1, top2, best, gap, e_gap, wden, wtop1, wtop2 = (
            sb(name, [P, BT]) for name in ("top1", "top2", "best", "gap", "e_gap", "wden", "wtop1", "wtop2"))
        w16 = sb("w16", [P, TILES, 2 * EXPERTS], f16)
        wT16 = sb("wT16", [2 * EXPERTS, TOKENS], f16)

        def pair(big, k):
            return big[:, k * 2 * CT:(k + 1) * 2 * CT, :].rearrange("p (j t) d -> p j (t d)", j=2)

        g_c, g_s = pair(gate0, 0), pair(gate0, 1)
        u_b, u_c = pair(x_sb, 0), pair(x_sb, 1)
        glu, act32, actw = yT[:, 0:2, :], yT[:, 2:4, :], hT32
        o_th = sb("o_th", [P, CHUNK])
        gT = sb("gT", [P, CHUNK])
        prodT = sb("prodT", [P, CHUNK])

        S = [ctx.enter_context(nc.psum_tensor(f"S{i}", [P, 2 * CHUNK], f32)) for i in range(2)]
        T0, T1, O, X = (ctx.enter_context(nc.psum_tensor(n, [P, CHUNK], f32))[:, :]
                        for n in ("T0", "T1", "O", "X"))
        T = (T0, T1)
        SH = [S[0][:, 0:CHUNK], S[0][:, CHUNK:2 * CHUNK], S[1][:, 0:CHUNK], S[1][:, CHUNK:2 * CHUNK]]

        USES = ([("rt", 0, 0)]
                + [(k, j, s) for j in range(2)
                   for k, s in (("dk", 0), ("q", 0), ("q", 1), ("dv", 0), ("v1", 0))]
                + [("hs", j, s) for j in range(2) for s in range(2)] + [("wt", 0, 0)]
                + [("out", j, s) for j in range(2) for s in range(2)])
        RING = (SH[0], SH[1], SH[2], SH[3], X, T1)
        BY_DVE = ("rt", "q", "wt")

        def use_of(kind, j=0, s=0):
            n = USES.index((kind, j, s))
            return n, RING[n % len(RING)]

        def reads_until(n):
            dve = sum(k in BY_DVE for k, _, _ in USES[:n + 1])
            return n + 1 - dve, dve

        x_in = [sem(f"x_in{c}") for c in range(CHUNKS)]
        out_done = sem("out_done")
        dve_self, pool_self = sem("dve_self"), sem("pool_self")
        (w0_in, vecs_in, ffn1_in, ffn2_in, l1_in, consts_ready, fc1_ready, fc1_hi_ready, fc1_lo_ready,
         fc2_ready, wv_ready, A_ready, A_hi_ready, A_lo_ready, scales_ready, xn_ready, hz_ready,
         xt_done, ht_done, xt_hi_ready, xt_lo_ready, h32_ready, h_hi_ready, h_lo_ready, xnb_ready,
         fc1_done, y_ready, fc2_done, u_ready, gate0_ready, k_done, k_hi_ready, k_lo_ready,
         v_done, v_hi_ready, v_lo_ready, s_done, max_ready, exp_done, pt_done, pt_hi_ready,
         pt_lo_ready, o_done, o_read, x1_ready, stats_ready, seed_ready, x1n_ready, dxn_ready, l1w_ready,
         x1t_done, x1t_hi, x1t_lo, router_done, logits_read, gap_ready, egap_ready, w16_ready,
         wt_done, wt_ready, use_done, use_act, use_dve, adv_ready, ctx_ready,
         gate_done, up_done, wb_done, down_done, gc_ready, gs_ready, ub_ready, uc_ready, glu_ready,
         act_ready, actw_ready, oth_ready, gt_ready, prod_ready, turned, x2_ready) = (
            sem(n) for n in (
                "w0_in vecs_in ffn1_in ffn2_in l1_in consts_ready fc1_ready fc1_hi_ready fc1_lo_ready "
                "fc2_ready wv_ready A_ready A_hi_ready A_lo_ready scales_ready xn_ready hz_ready "
                "xt_done ht_done xt_hi_ready xt_lo_ready h32_ready h_hi_ready h_lo_ready xnb_ready "
                "fc1_done y_ready+ fc2_done u_ready gate0_ready+ k_done k_hi_ready k_lo_ready+ "
                "v_done v_hi_ready v_lo_ready+ s_done max_ready exp_done pt_done pt_hi_ready "
                "pt_lo_ready o_done o_read x1_ready stats_ready seed_ready x1n_ready dxn_ready l1w_ready "
                "x1t_done x1t_hi x1t_lo router_done logits_read gap_ready egap_ready w16_ready "
                "wt_done wt_ready use_done use_act use_dve adv_ready ctx_ready "
                "gate_done up_done wb_done down_done gc_ready gs_ready ub_ready uc_ready glu_ready "
                "act_ready actw_ready oth_ready gt_ready prod_ready turned x2_ready").split())

        block = ctx.enter_context(nc.Block())

        def bc(ap, n):
            return ap.unsqueeze(2).broadcast_to([P, ap.shape[1], n])

        def tiles_of(bank):
            return bank.rearrange("p (t d) -> p t d", d=P)

        def chunk(c):
            return ds(c * CHUNK, CHUNK)

        def before(c, e, lag):
            return (c, e - lag) if e >= lag else (c - 1, e - lag + EXPERTS)

        def exists(c):
            return not isinstance(c, int) or c >= 0

        def at_least(c, k):
            return c >= k if isinstance(c, int) else True

        @block.sync
        def _(sp):
            for c in range(CHUNKS):
                sp.dma_start(x_sb[:, c * CT:(c + 1) * CT, :],
                             x_rows[:, c * CT:(c + 1) * CT, :]).then_inc(x_in[c], 16)
            for dst, src in ((q2_sb[:, :, :], q2), (s2_sb[:, :, :], s2.partition_broadcast(P)),
                             (b2_sb[:, :], b2.partition_broadcast(P))):
                sp.dma_start(dst, src).then_inc(ffn2_in, 16)
            sp.wait_ge(xn_ready, 1)
            for dst, src in ((w1_sb[:, :], w1s), (gup_sb[:, :, :, :], gup),
                             (down_sb[:, :, :], down), (db_sb[:, :], db)):
                sp.dma_start(dst, src).then_inc(l1_in, 16)
            with sp.Fori(0, CHUNKS) as c:
                sp.wait_ge(x2_ready, c + 1)
                sp.dma_start(out_rows[:, ds(c * CT, CT), :],
                             x1[:, ds(c * CT, CT), :]).then_inc(out_done, 16)
            sp.wait_ge(out_done, 16 * CHUNKS)

        @block.gpsimd
        def _(pool):
            g = nc.gpsimd
            n_self = [0]

            def link(ins):
                n_self[0] += 1
                ins.then_inc(pool_self, 1)
                pool.wait_ge(pool_self, n_self[0])

            def diagonal(ap, base, pattern, fill=1.0):
                return g.affine_select(out=ap, in_=ap, compare_op=ALU.not_equal, fill=fill,
                                       base=base, pattern=pattern, channel_multiplier=1)

            link(g.memset(ident[:, :], 0.0))
            diagonal(ident[:, :], 0, [[-1, P]]).then_inc(consts_ready, 1)

            pool.wait_ge(ffn2_in, 16 * 3)
            link(g.tensor_scalar(fc2_w[:, :, :], q2_sb[:, :, :], -ZERO_POINT, None, ALU.add))
            g.tensor_tensor(fc2_w[:, :, :], fc2_w[:, :, :], s2_sb[:, :, :],
                            ALU.mult).then_inc(fc2_ready, 1)
            pool.wait_ge(fc1_hi_ready, 1)
            g.tensor_tensor(fc1_lo[:, :], fc1_w[:, :], fc1_hi[:, :],
                            ALU.subtract).then_inc(fc1_lo_ready, 1)
            g.tensor_tensor(wv_lo[:, :], w0_sb[:, WVT, :], wv_hi[:, :],
                            ALU.subtract).then_inc(wv_ready, 1)
            link(g.tensor_scalar(b2_sb[:, :], b2_sb[:, :], 0.5, None, ALU.mult))

            with pool.Fori(0, CHUNKS // 2) as half:
                for j in range(2):
                    c = 2 * half + j
                    pool.wait_ge(h_hi_ready, c + 1)
                    g.tensor_tensor(hT_lo[:, chunk(c)], hT32[:, j, :], hT_hi[:, chunk(c)],
                                    ALU.subtract).then_inc(h_lo_ready, 1)
                    pool.wait_ge(xn_ready, CT * (c + 1))
                    g.tensor_tensor(xnb[:, ds(c * CT, CT), :], xn[:, ds(c * CT, CT), :],
                                    b2_sb[:, :].unsqueeze(1).broadcast_to([P, CT, P]),
                                    ALU.add).then_inc(xnb_ready, 1)

            g.memset(ident16[:, :], 0.0)
            g.memset(headsum[:, :], 1.0)
            for e in range(EXPERTS):
                g.memset(rank[:, e:e + 1], float(EXPERTS - e))
            link(g.memset(sel16[:, :, :], 0.0))
            diagonal(ident16[:, :], 0, [[-1, P]])
            link(diagonal(sel16[:, :, :], 0, [[-1, EXPERTS], [0, P]], 0.5))
            diagonal(sel16[:, :, :], -EXPERTS, [[-1, EXPERTS], [0, P]], 0.5)
            hs = headsum[:, :].rearrange("p (h d) -> p h d", d=HD)
            link(g.affine_select(out=hs, in_=hs, compare_op=ALU.is_ge, fill=0.0, base=0,
                                 pattern=[[-HD, HEADS], [0, HD]], channel_multiplier=1))
            g.affine_select(out=hs, in_=hs, compare_op=ALU.is_ge, fill=0.0, base=HD - 1,
                            pattern=[[HD, HEADS], [0, HD]], channel_multiplier=-1)
            pool.wait_ge(l1_in, 16 * 4)
            g.tensor_scalar(ub1[:, :], vecs_sb[:, UB:UB + EXPERTS], 1.0, None, ALU.add)
            g.tensor_scalar(bo_half[:, :], vecs_sb[:, BO:BO + 1], 0.5, None, ALU.mult)
            g.tensor_copy(db_hi[:, :], db_sb[:, :])
            link(g.tensor_copy(w1_hi[:, :], w1_sb[:, :]))
            g.tensor_tensor(w1_lo[:, :], w1_sb[:, :], w1_hi[:, :], ALU.subtract)
            g.tensor_tensor(db_lo[:, :], db_sb[:, :], db_hi[:, :], ALU.subtract).then_inc(l1w_ready, 1)

            def residual(t, j):
                pool.wait_ge(o_read, t + 1)
                g.tensor_tensor(x1[:, ds(t, 1), :], sg0[:, j:j + 1, :], x_sb[:, ds(t, 1), :],
                                ALU.add).then_inc(x1_ready, 1)

            with pool.Fori(0, BT // 2) as half:
                for j in range(2):
                    t = 2 * half + j
                    g.tensor_copy(gup_hi[:, ds(t, 1), :, :], gup_sb[:, ds(t, 1), :, :])\
                        .then_inc(l1w_ready, 1)
                    pool.wait_ge(l1w_ready, 2 * t + 2)
                    g.tensor_tensor(gup_lo[:, ds(t, 1), :, :], gup_sb[:, ds(t, 1), :, :],
                                    gup_hi[:, ds(t, 1), :, :], ALU.subtract).then_inc(l1w_ready, 1)
                    residual(t, j)

            def newton(b):
                r = slice(b * BT, (b + 1) * BT)
                pool.wait_ge(seed_ready, b + 1)
                src = seed[:, r].bitcast(f32)
                for k in range(3):
                    link(g.tensor_tensor(newt[:, r], src, src, ALU.mult))
                    link(g.tensor_tensor(newt2[:, r], newt[:, r], half_a[:, r], ALU.mult))
                    link(g.tensor_scalar(newt[:, r], newt2[:, r], 1.5, None, ALU.add))
                    link(g.tensor_tensor(rs1[:, r], newt[:, r], src, ALU.mult))
                    src = rs1[:, r]

            def norm(t0, t1):
                for t in range(t0, t1):
                    g.tensor_scalar(x1n[:, t, :], x1[:, t, :], mv1[:, t, 0:1], rs1[:, t:t + 1],
                                    ALU.subtract, ALU.mult).then_inc(x1n_ready, 1)

            residual(BT, 0)
            newton(0)
            residual(BT + 1, 1)
            norm(0, CT)
            residual(BT + 2, 0)
            norm(CT, 2 * CT)
            residual(BT + 3, 1)
            with pool.Fori(BT // 2 + 2, TILES // 2) as half:
                for j in range(2):
                    residual(2 * half + j, j)

            def product(c, e):
                n = EXPERTS * c + e
                pool.wait_ge(uc_ready, n + 1)
                if at_least(c, 1) or e >= 2:
                    pool.wait_ge(actw_ready, n - 1)
                g.tensor_tensor(act32[:, e % 2, :], u_c[:, e % 2, :], glu[:, e % 2, :],
                                ALU.mult).then_inc(act_ready, 1)

            def gate_rows(c):
                pool.wait_ge(gt_ready, c + 1)
                if at_least(c, 1):
                    pool.wait_ge(turned, c)
                g.tensor_tensor(prodT[:, :], gT[:, :], sT[:, chunk(c)], ALU.mult).then_inc(prod_ready, 1)

            def differences(j):
                pool.wait_ge(x1n_ready, BT + CT * (j + 1))
                r = slice(j * CT, (j + 1) * CT)
                g.tensor_tensor(dxn[:, r, :], x1n[:, r, :], x1n[:, BT + j * CT:BT + (j + 1) * CT, :],
                                ALU.subtract).then_inc(dxn_ready, 1)

            newton(1)
            norm(BT, BT + 2)
            for e in range(EXPERTS - 1):
                product(0, e)
                if e < 3:
                    norm(BT + 2 + 2 * e, BT + 4 + 2 * e)
                elif e < 5:
                    differences(e - 3)
            for j in range(2):
                for s in range(2):
                    pool.wait_ge(adv_ready, 2 * j + s + 1)
                    pool.wait_ge(use_act, reads_until(use_of("v1", j)[0])[0])
                    g.tensor_tensor(ctxT[j][:, s, :], adv[j][:, s, :], v1T[:, j, :],
                                    ALU.add).then_inc(ctx_ready, 1)
            with pool.Fori(1, CHUNKS) as c:
                for e in range(EXPERTS):
                    product(*before(c, e, 1))
                    if e == 4:
                        gate_rows(c - 1)
            product(CHUNKS - 1, EXPERTS - 1)
            gate_rows(CHUNKS - 1)

        @block.scalar
        def _(act):
            a = nc.scalar
            act.dma_start(w0_sb[:, :, :], w0).then_inc(w0_in, 16)
            act.dma_start(vecs_sb[:, :], vecs).then_inc(vecs_in, 16)
            for dst, src in ((q1_sb[:, :], q1), (s1_sb[:, :], s1.partition_broadcast(P))):
                act.dma_start(dst, src).then_inc(ffn1_in, 16)

            act.wait_ge(vecs_in, 16)
            a.activation(scratch[:, :], vecs_sb[:, 0:1], ACT.Silu).then_inc(y_ready, FB)
            act.wait_ge(A_ready, 1)
            a.copy(A_hi[:, :], SH[0][:, 0:P]).then_inc(A_hi_ready, 1)
            a.copy(wv_hi[:, :], w0_sb[:, WVT, :])
            act.wait_ge(fc1_ready, 1)
            a.copy(fc1_hi[:, :], fc1_w[:, :]).then_inc(fc1_hi_ready, 1)

            def second_norm(c):
                for t in range(c * CT, (c + 1) * CT):
                    ins = a.activation(hz[:, t, :], x_sb[:, t, :], ACT.Identity,
                                       bias=hz_bias[:, t:t + 1], scale=rs[:, 1, t:t + 1])
                ins.then_inc(hz_ready, 1)

            def columns(c, slot):
                act.wait_ge(xt_done, c + 1)
                a.copy(xT_hi[:, chunk(c)], T0).then_inc(xt_hi_ready, 1)
                act.wait_ge(ht_done, c + 1)
                if not isinstance(c, int) or c >= 2:
                    act.wait_ge(h_lo_ready, c - 1)
                a.activation(hT32[:, slot, :], T1, ACT.Identity, bias=vecs_sb[:, BETA:BETA + 1],
                             scale=vecs_sb[:, GAMMA:GAMMA + 1]).then_inc(h32_ready, 1)

            act.wait_ge(scales_ready, 1)
            second_norm(0)
            columns(0, 0)
            for c in range(1, CHUNKS):
                second_norm(c)

            def ffn(c, following):
                for i, f in enumerate(F_ORDER):
                    act.wait_ge(fc1_done, FB * c + i + 1)
                    a.activation(yT[:, f, :], SH[f], ACT.Silu,
                                 bias=vecs_sb[:, FC1B + f:FC1B + f + 1]).then_inc(y_ready, 1)
                if following is not None:
                    columns(c + 1, following)
                act.wait_ge(k_done, c + 1)
                a.copy(kT_hi[:, chunk(c)], O).then_inc(k_hi_ready, 1)
                act.wait_ge(v_done, c + 1)
                a.activation(v_hi[:, ds(c * CT, CT), :], tiles_of(X), ACT.Copy,
                             scale=NORM_FACT).then_inc(v_hi_ready, 1)
                act.wait_ge(u_ready, c + 1)
                a.activation(gate0[:, ds(c * CT, CT), :], tiles_of(u0[:, :]),
                             ACT.Silu).then_inc(gate0_ready, 1)

            ffn(0, 1)
            ffn(1, 0)
            ffn(2, 1)
            ffn(3, None)

            def exp(t, j):
                act.wait_ge(max_ready, t + 1)
                a.activation(probs[:, j, :], S[j][:, :], ACT.Exp, bias=neg_max[:, ds(t, 1)],
                             accum_out=row_sum[:, ds(t, 1)]).then_inc(exp_done, 1)

            def split_hi(t, j):
                for h in range(2):
                    act.wait_ge(pt_done, 2 * t + h + 1)
                    a.copy(pT_hi[:, j, h * CHUNK:(h + 1) * CHUNK], T[h]).then_inc(pt_hi_ready, 1)

            def layer1_columns(c, bank):
                act.wait_ge(x1t_done, c + 1)
                a.copy(x1T_hi[:, chunk(c)], bank).then_inc(x1t_hi, 1)

            def gap_exp(b):
                act.wait_ge(gap_ready, b + 1)
                a.activation(e_gap[:, :], gap[:, :], ACT.Exp).then_inc(egap_ready, 1)

            exp(0, 0)
            with act.Fori(0, (TILES - 2) // 2) as half:
                for j in range(2):
                    split_hi(2 * half + j, j)
                    exp(2 * half + j + 1, 1 - j)
            split_hi(TILES - 2, 0)
            exp(TILES - 1, 1)
            for c in range(2):
                layer1_columns(c, (X, SH[0])[c])
            split_hi(TILES - 1, 1)

            def expert(c, e):
                n = EXPERTS * c + e
                late = at_least(c, 1) or e >= 2
                act.wait_ge(gc_ready, n + 1)
                if late:
                    act.wait_ge(glu_ready, n - 1)
                a.activation(g_s[:, e % 2, :], g_c[:, e % 2, :], ACT.Tanh,
                             scale=0.5 * ALPHA).then_inc(gs_ready, 1)
                act.wait_ge(up_done, n + 1)
                if late:
                    act.wait_ge(uc_ready, n - 1)
                a.activation(u_b[:, e % 2, :], SH[2 + e % 2], ACT.Identity,
                             bias=ub1[:, e:e + 1]).then_inc(ub_ready, 1)

            def finish(c):
                act.wait_ge(down_done, EXPERTS * (c + 1))
                if at_least(c, 1):
                    act.wait_ge(gt_ready, c)
                a.activation(o_th[:, :], O, ACT.Tanh, scale=0.5).then_inc(oth_ready, 1)

            gap_exp(0)
            for e in range(EXPERTS):
                expert(0, e)
                if e >= 4:
                    layer1_columns(e - 2, X)

            for n, (kind, j, s) in enumerate(USES):
                if kind in BY_DVE:
                    continue
                bank = RING[n % len(RING)]
                act.wait_ge(use_done, n + 1)
                if kind == "dk":
                    ins = a.copy(dkT[:, j, :], bank)
                elif kind == "dv":
                    ins = a.activation(dvT[:, j, :], bank, ACT.Copy, scale=0.5)
                elif kind == "v1":
                    ins = a.activation(v1T[:, j, :], bank, ACT.Identity, bias=vecs_sb[:, BV:BV + 1])
                elif kind == "hs":
                    ins = a.activation(th[j][:, s, :], bank, ACT.Tanh, scale=0.5 * HEAD_SCALE)
                else:
                    ins = a.activation(sT[:, chunk(j + 2 * s)], bank, ACT.Identity,
                                       bias=bo_half[:, :], scale=0.5)
                ins.then_inc(use_act, 1)
                if (kind, j) == ("v1", 0):
                    gap_exp(1)

            with act.Fori(1, CHUNKS) as c:
                for e in range(EXPERTS):
                    expert(c, e)
                    if e == 2:
                        finish(c - 1)
            finish(CHUNKS - 1)

        @block.vector
        def _(dve):
            v = nc.vector
            n_self = [0]

            def link(ins):
                n_self[0] += 1
                ins.then_inc(dve_self, 1)
                dve.wait_ge(dve_self, n_self[0])

            def rsqrt_seed(a_, r):
                v.tensor_scalar(half_a[:, r], a_, -0.5, None, ALU.mult)
                link(v.tensor_scalar(seed[:, r], a_.bitcast(i32), 1, None, ALU.logical_shift_right))
                return v.tensor_scalar(seed[:, r], seed[:, r], -1.0, RSQRT_MAGIC, ALU.mult, ALU.add)

            v.memset(scratch_dve[:, 0:1], 0.0).then_inc(k_lo_ready, 1)
            v.memset(scratch_dve[:, 1:2], 0.0).then_inc(v_lo_ready, 1)
            v.memset(scratch_dve[:, 2:3], 0.0).then_inc(gate0_ready, 1)

            for c in range(CHUNKS):
                dve.wait_ge(x_in[c], 16)
                for t in range(c * CT, (c + 1) * CT):
                    ins = v.bn_stats(stats[:, t, :], x_sb[:, t, :])
            link(ins)
            for t in range(TILES):
                ins = v.bn_aggr(mv[:, t, :], stats[:, t, :])
            link(ins)
            link(v.tensor_scalar(rs_arg[:, 0, :], mv[:, :, 1], EPS, None, ALU.add))
            link(v.scalar_tensor_tensor(rs_arg[:, 1, :], rs_arg[:, 0, :], EPS, mv[:, :, 1],
                                        ALU.mult, ALU.add))
            both = slice(0, 2 * TILES)
            link(rsqrt_seed(rs_arg[:, :, :].rearrange("p a t -> p (a t)"), both))
            src = seed[:, both].bitcast(f32)
            y = rs[:, :, :].rearrange("p a t -> p (a t)")
            for k in range(3):
                link(v.tensor_tensor(newt[:, both], src, src, ALU.mult))
                link(v.tensor_tensor(newt2[:, both], newt[:, both], half_a[:, both], ALU.mult))
                link(v.scalar_tensor_tensor(y, newt2[:, both], 1.5, src, ALU.add, ALU.mult))
                src = y
            v.scalar_tensor_tensor(hz_bias[:, :], mv[:, :, 0], -1.0, rs[:, 1, :], ALU.mult,
                                   ALU.mult).then_inc(scales_ready, 1)

            def norm(c):
                for t in range(c * CT, (c + 1) * CT):
                    v.tensor_scalar(xn[:, t, :], x_sb[:, t, :], mv[:, t, 0:1], rs[:, 0, t:t + 1],
                                    ALU.subtract, ALU.mult).then_inc(xn_ready, 1)

            def columns(c, slot):
                dve.wait_ge(xt_hi_ready, c + 1)
                v.tensor_tensor(xT_lo[:, chunk(c)], T0, xT_hi[:, chunk(c)],
                                ALU.subtract).then_inc(xt_lo_ready, 1)
                dve.wait_ge(h32_ready, c + 1)
                v.tensor_copy(hT_hi[:, chunk(c)], hT32[:, slot, :]).then_inc(h_hi_ready, 1)

            norm(0)
            dve.wait_ge(ffn1_in, 32)
            v.scalar_tensor_tensor(fc1_w[:, :], q1_sb[:, :], -ZERO_POINT, s1_sb[:, :], ALU.add,
                                   ALU.mult).then_inc(fc1_ready, 1)
            dve.wait_ge(A_hi_ready, 1)
            v.tensor_tensor(A_lo[:, :], SH[0][:, 0:P], A_hi[:, :], ALU.subtract).then_inc(A_lo_ready, 1)
            norm(1)
            columns(0, 0)
            norm(2)
            norm(3)

            def ffn(c, following):
                if following is not None:
                    columns(c + 1, following)
                dve.wait_ge(k_hi_ready, c + 1)
                v.tensor_tensor(kT_lo[:, chunk(c)], O, kT_hi[:, chunk(c)],
                                ALU.subtract).then_inc(k_lo_ready, 1)
                dve.wait_ge(v_hi_ready, c + 1)
                v.scalar_tensor_tensor(v_lo[:, ds(c * CT, CT), :], tiles_of(X), NORM_FACT,
                                       v_hi[:, ds(c * CT, CT), :], ALU.mult,
                                       ALU.subtract).then_inc(v_lo_ready, 1)
                dve.wait_ge(fc2_done, c + 1)
                dve.wait_ge(xnb_ready, c + 1)
                dve.wait_ge(gate0_ready, c + 1)
                v.scalar_tensor_tensor(tiles_of(u0[:, :]), tiles_of(SH[0]), 0.5,
                                       xnb[:, ds(c * CT, CT), :], ALU.mult, ALU.add).then_inc(u_ready, 1)

            ffn(0, 1)
            ffn(1, 0)
            ffn(2, 1)
            ffn(3, None)

            def row_max(t, j):
                dve.wait_ge(s_done, t + 1)
                v.tensor_reduce(neg_max[:, ds(t, 1)], S[j][:, :], AX.X, ALU.max,
                                negate=True).then_inc(max_ready, 1)

            def split_lo(t, j):
                dve.wait_ge(exp_done, t + 1)
                v.reciprocal(row_inv[:, ds(t, 1)], row_sum[:, ds(t, 1)])
                for h in range(2):
                    r = slice(h * CHUNK, (h + 1) * CHUNK)
                    dve.wait_ge(pt_hi_ready, 2 * t + h + 1)
                    v.tensor_tensor(pT_lo[:, j, r], T[h], pT_hi[:, j, r],
                                    ALU.subtract).then_inc(pt_lo_ready, 1)

            def gated_rows(t, j):
                dve.wait_ge(o_done, t + 1)
                v.scalar_tensor_tensor(sg0[:, j:j + 1, :], O[:, 0:P].unsqueeze(1),
                                       row_inv[:, ds(t, 1)], gate0[:, ds(t, 1), :],
                                       ALU.mult, ALU.mult).then_inc(o_read, 1)

            def statistics(t):
                dve.wait_ge(x1_ready, t + 1)
                v.bn_stats(stats1[:, ds(t, 1), :].rearrange("p a b -> p (a b)"),
                           x1[:, ds(t, 1), :].rearrange("p a b -> p (a b)")).then_inc(stats_ready, 1)

            def layer1_scale(b):
                r = slice(b * BT, (b + 1) * BT)
                dve.wait_ge(stats_ready, BT * (b + 1))
                for t in range(b * BT, (b + 1) * BT):
                    ins = v.bn_aggr(mv1[:, t, :], stats1[:, t, :])
                link(ins)
                link(v.tensor_scalar(rs1_arg[:, r], mv1[:, r, 1], EPS, None, ALU.add))
                rsqrt_seed(rs1_arg[:, r], r).then_inc(seed_ready, 1)

            def layer1_columns(c, bank):
                dve.wait_ge(x1t_hi, c + 1)
                v.tensor_tensor(x1T_lo[:, chunk(c)], bank, x1T_hi[:, chunk(c)],
                                ALU.subtract).then_inc(x1t_lo, 1)

            def body(t, j):
                row_max(t + 1, 1 - j)
                split_lo(t, j)
                if not isinstance(t, int) or t >= 1:
                    gated_rows(t - 1, 1 - j)
                if not isinstance(t, int) or t >= 2:
                    statistics(t - 2)

            dve.wait_ge(gate0_ready, CHUNKS + 1)
            row_max(0, 0)
            body(0, 0)
            body(1, 1)
            with dve.Fori(1, BT // 2) as half:
                for j in range(2):
                    body(2 * half + j, j)
            body(BT, 0)
            body(BT + 1, 1)
            layer1_scale(0)
            with dve.Fori(BT // 2 + 1, TILES // 2 - 1) as half:
                for j in range(2):
                    body(2 * half + j, j)
            t = TILES - 2
            row_max(t + 1, 1)
            split_lo(t, 0)
            gated_rows(t - 1, 1)
            statistics(t - 2)
            for c in range(2):
                layer1_columns(c, (X, SH[0])[c])
            split_lo(t + 1, 1)
            gated_rows(t, 0)
            statistics(t - 1)

            def top_two(b, bank, read):
                lg, l2 = logits[:, :, :], logits2[:, :, :]
                v.tensor_copy(lg, bank[:, 0:BT * EXPERTS].rearrange("p (t e) -> p t e", e=EXPERTS))\
                    .then_inc(read, 1)
                dve.wait_ge(read, 1)
                rank_b = rank[:, :].unsqueeze(1).broadcast_to(BE)
                for src, top, one_hot in ((lg, top1, first), (l2, top2, second)):
                    link(v.tensor_reduce(top[:, :], src, AX.X, ALU.max))
                    link(v.tensor_tensor(equal[:, :, :], src, bc(top[:, :], EXPERTS), ALU.is_equal))
                    link(v.tensor_tensor(ranked[:, :, :], equal[:, :, :], rank_b, ALU.mult))
                    link(v.tensor_reduce(best[:, :], ranked[:, :, :], AX.X, ALU.max))
                    link(v.tensor_tensor(one_hot[:, :, :], ranked[:, :, :], bc(best[:, :], EXPERTS),
                                         ALU.is_equal))
                    if one_hot is first:
                        link(v.scalar_tensor_tensor(l2, first[:, :, :], LOWEST, lg, ALU.mult, ALU.add))
                v.tensor_tensor(gap[:, :], top2[:, :], top1[:, :], ALU.subtract).then_inc(gap_ready, 1)

            def weights_of_two(b):
                dve.wait_ge(egap_ready, b + 1)
                link(v.tensor_scalar(wden[:, :], e_gap[:, :], 1.0, None, ALU.add))
                link(v.reciprocal(wtop1[:, :], wden[:, :]))
                link(v.tensor_tensor(wtop2[:, :], wtop1[:, :], e_gap[:, :], ALU.mult))
                v.tensor_tensor(first[:, :, :], first[:, :, :], bc(wtop1[:, :], EXPERTS), ALU.mult)
                link(v.tensor_tensor(second[:, :, :], second[:, :, :], bc(wtop2[:, :], EXPERTS), ALU.mult))
                link(v.tensor_tensor(wrow[:, :, :], first[:, :, :], second[:, :, :], ALU.add))
                hi = w16[:, b * BT:(b + 1) * BT, 0:EXPERTS]
                link(v.tensor_copy(hi, wrow[:, :, :]))
                v.tensor_tensor(w16[:, b * BT:(b + 1) * BT, EXPERTS:2 * EXPERTS], wrow[:, :, :], hi,
                                ALU.subtract).then_inc(w16_ready, 1)

            dve.wait_ge(router_done, 1)
            top_two(0, SH[1], logits_read)
            gated_rows(t + 1, 1)
            statistics(t)
            weights_of_two(0)

            def clip_gate(c, e):
                n = EXPERTS * c + e
                if at_least(c, 1) or e >= 2:
                    dve.wait_ge(glu_ready, n - 1)
                dve.wait_ge(gate_done, n + 1)
                v.tensor_scalar(g_c[:, e % 2, :], SH[e % 2], vecs_sb[:, GB + e:GB + e + 1], LIMIT,
                                ALU.add, ALU.min).then_inc(gc_ready, 1)

            def gated_and_up(c, e):
                n = EXPERTS * c + e
                dve.wait_ge(gs_ready, n + 1)
                v.scalar_tensor_tensor(glu[:, e % 2, :], g_s[:, e % 2, :], 1.0, g_c[:, e % 2, :],
                                       ALU.add, ALU.mult).then_inc(glu_ready, 1)
                dve.wait_ge(ub_ready, n + 1)
                v.tensor_scalar(u_c[:, e % 2, :], u_b[:, e % 2, :], LIMIT + 1.0, 1.0 - LIMIT,
                                ALU.min, ALU.max).then_inc(uc_ready, 1)

            def weigh(c, e):
                n = EXPERTS * c + e
                dve.wait_ge(act_ready, n + 1)
                dve.wait_ge(wb_done, n + 1)
                if at_least(c, 1) or e >= 2:
                    dve.wait_ge(down_done, n - 1)
                v.tensor_tensor(actw[:, e % 2, :], act32[:, e % 2, :], T[e % 2],
                                ALU.mult).then_inc(actw_ready, 1)

            def step(c, e):
                clip_gate(c, e)
                if exists(before(c, e, 1)[0]):
                    gated_and_up(*before(c, e, 1))
                if exists(before(c, e, 2)[0]):
                    weigh(*before(c, e, 2))

            def gate_columns(c):
                dve.wait_ge(oth_ready, c + 1)
                if at_least(c, 1):
                    dve.wait_ge(prod_ready, c)
                v.scalar_tensor_tensor(gT[:, :], o_th[:, :], 1.0, O, ALU.add, ALU.mult)\
                    .then_inc(gt_ready, 1)

            def last_rows(c):
                dve.wait_ge(turned, c + 1)
                r = ds(c * CT, CT)
                v.tensor_tensor(x1[:, r, :], tiles_of(X), x1[:, r, :], ALU.add).then_inc(x2_ready, 1)

            for e in range(EXPERTS):
                clip_gate(0, e)
                if e == 0:
                    statistics(TILES - 1)
                    layer1_scale(1)
                if e == 1:
                    dve.wait_ge(wt_done, 1)
                    v.tensor_copy(wT16[:, 0:KEYS], X[0:2 * EXPERTS, :].bitcast(f16)).then_inc(wt_ready, 1)
                if e >= 1:
                    gated_and_up(0, e - 1)
                if e >= 2:
                    weigh(0, e - 2)
                if e >= 5:
                    layer1_columns(e - 3, X)
            layer1_columns(EXPERTS - 3, X)

            def scores(j):
                dve.wait_ge(use_act, reads_until(use_of("dk", j)[0])[0])
                for s in range(2):
                    n, bank = use_of("q", j, s)
                    dve.wait_ge(use_done, n + 1)
                    v.scalar_tensor_tensor(qk[j][:, s, :], bank, vecs_sb[:, BQ:BQ + 1], dkT[:, j, :],
                                           ALU.add, ALU.mult).then_inc(use_dve, 1)

            n, bank = use_of("rt")
            dve.wait_ge(use_done, n + 1)
            top_two(1, bank, use_dve)
            scores(0)
            weights_of_two(1)
            scores(1)
            for j in range(2):
                for s in range(2):
                    dve.wait_ge(use_act, reads_until(use_of("hs", j, s)[0])[0])
                    v.scalar_tensor_tensor(adv[j][:, s, :], th[j][:, s, :], 1.0, dvT[:, j, :],
                                           ALU.add, ALU.mult).then_inc(adv_ready, 1)
            n, bank = use_of("wt")
            dve.wait_ge(use_done, n + 1)
            v.tensor_copy(wT16[:, KEYS:2 * KEYS], bank[0:2 * EXPERTS, :].bitcast(f16)).then_inc(use_dve, 1)

            with dve.Fori(1, CHUNKS) as c:
                for e in range(EXPERTS):
                    step(c, e)
                    if e == 3:
                        gate_columns(c - 1)
                    if e == 7:
                        last_rows(c - 1)
            gated_and_up(CHUNKS - 1, EXPERTS - 1)
            weigh(CHUNKS - 1, EXPERTS - 2)
            weigh(CHUNKS - 1, EXPERTS - 1)
            gate_columns(CHUNKS - 1)
            last_rows(CHUNKS - 1)

        @block.tensor
        def _(pe):
            mm = nc.tensor.matmul

            def three(o, l_hi, l_lo, r_hi, r_lo):
                mm(o, l_hi, r_hi, start=True, stop=False)
                mm(o, l_hi, r_lo, start=False, stop=False)
                return mm(o, l_lo, r_hi, start=False, stop=True)

            def turn_tiles(bank, src, first):
                for k in range(CT):
                    ins = nc.tensor.transpose(bank[:, k * P:(k + 1) * P], src[:, first + k, :], ident[:, :])
                return ins

            pe.wait_ge(w0_in, 16)
            mm(SH[0][:, 0:P], w0_sb[:, WK, :], w0_sb[:, WQ, :], start=True, stop=True).then_inc(A_ready, 1)

            def columns(c):
                pe.wait_ge(xn_ready, CT * (c + 1))
                if c:
                    pe.wait_ge(xt_lo_ready, c)
                turn_tiles(T0, xn, CT * c).then_inc(xt_done, 1)
                pe.wait_ge(hz_ready, c + 1)
                if c:
                    pe.wait_ge(h32_ready, c)
                turn_tiles(T1, hz, CT * c).then_inc(ht_done, 1)

            pe.wait_ge(consts_ready, 1)
            columns(0)

            for c in range(CHUNKS):
                cols = chunk(c)
                if c == 0:
                    for ready in (fc1_lo_ready, A_lo_ready):
                        pe.wait_ge(ready, 1)
                pe.wait_ge(h_lo_ready, c + 1)
                pe.wait_ge(xt_lo_ready, c + 1)
                for i, f in enumerate(F_ORDER):
                    w = slice(f * P, (f + 1) * P)
                    pe.wait_ge(y_ready, FB * c + i + 1)
                    if f == 0 and c:
                        pe.wait_ge(u_ready, c)
                    three(SH[f], fc1_hi[:, w], fc1_lo[:, w], hT_hi[:, cols],
                          hT_lo[:, cols]).then_inc(fc1_done, 1)
                if c + 1 < CHUNKS:
                    columns(c + 1)
                pe.wait_ge(k_lo_ready, c + 1)
                three(O, A_hi[:, :], A_lo[:, :], xT_hi[:, cols], xT_lo[:, cols]).then_inc(k_done, 1)
                pe.wait_ge(v_lo_ready, c + 1)
                pe.wait_ge(wv_ready, 1)
                for k in range(CT):
                    tok = ds(c * CHUNK + k * P, P)
                    ins = three(X[:, k * P:(k + 1) * P], xT_hi[:, tok], xT_lo[:, tok],
                                wv_hi[:, :], wv_lo[:, :])
                ins.then_inc(v_done, 1)
                pe.wait_ge(y_ready, FB * (c + 2))
                pe.wait_ge(fc2_ready, 1)
                for k in range(CT):
                    for f in range(FB):
                        ins = mm(SH[0][:, k * P:(k + 1) * P], yT[:, f, k * P:(k + 1) * P], fc2_w[:, f, :],
                                 start=(f == 0), stop=(f == FB - 1))
                ins.then_inc(fc2_done, 1)

            def logit(t, j, b):
                if not isinstance(t, int) or t >= 2:
                    pe.wait_ge(exp_done, t - 1)
                q = ds(t * P, P)
                for h in range(2):
                    keys = slice(b * KEYS + h * CHUNK, b * KEYS + (h + 1) * CHUNK)
                    ins = three(S[j][:, h * CHUNK:(h + 1) * CHUNK], xT_hi[:, q], xT_lo[:, q],
                                kT_hi[:, keys], kT_lo[:, keys])
                ins.then_inc(s_done, 1)

            def turn(t, j):
                pe.wait_ge(exp_done, t + 1)
                for h in range(2):
                    if not isinstance(t, int) or t >= 1:
                        pe.wait_ge(pt_lo_ready, 2 * t - 1 + h)
                    for k in range(CT):
                        at = h * CHUNK + k * P
                        ins = nc.tensor.transpose(T[h][:, k * P:(k + 1) * P], probs[:, j, at:at + P],
                                                  ident[:, :])
                    ins.then_inc(pt_done, 1)

            def weighted(t, j, b):
                if not isinstance(t, int) or t >= 1:
                    pe.wait_ge(o_read, t)
                for m in range(BT):
                    if m % CT == 0:
                        pe.wait_ge(pt_lo_ready, 2 * t + m // CT + 1)
                    at, vt = slice(m * P, (m + 1) * P), b * BT + m
                    for n, (l, r) in enumerate(((pT_hi, v_hi), (pT_hi, v_lo), (pT_lo, v_hi))):
                        ins = mm(O[:, 0:P], l[:, j, at], r[:, vt, :], start=(m == 0 and n == 0),
                                 stop=(m == BT - 1 and n == 2))
                ins.then_inc(o_done, 1)

            def body(t, j, b, b_logit):
                turn(t, j)
                if not isinstance(t, int) or t >= 1:
                    weighted(t - 1, 1 - j, b)
                if b_logit is not None:
                    logit(t + 2, j, b_logit)

            pe.wait_ge(k_lo_ready, CHUNKS + 1)
            pe.wait_ge(y_ready, FB * (CHUNKS + 1))
            pe.wait_ge(u_ready, CHUNKS)
            logit(0, 0, 0)
            logit(1, 1, 0)
            pe.wait_ge(v_lo_ready, CHUNKS + 1)
            body(0, 0, 0, 0)
            body(1, 1, 0, 0)
            with pe.Fori(1, BT // 2 - 1) as half:
                for j in range(2):
                    body(2 * half + j, j, 0, 0)
            body(BT - 2, 0, 0, 1)
            body(BT - 1, 1, 0, 1)
            body(BT, 0, 0, 1)
            body(BT + 1, 1, 1, 1)
            with pe.Fori(BT // 2 + 1, TILES // 2 - 1) as half:
                for j in range(2):
                    body(2 * half + j, j, 1, 1)

            def layer1_columns(c, bank, free, count):
                if c < CHUNKS:
                    pe.wait_ge(x1n_ready, CT * (c + 1))
                else:
                    pe.wait_ge(dxn_ready, c - CHUNKS + 1)
                pe.wait_ge(free, count)
                src, at = (x1n, CT * c) if c < CHUNKS else (dxn, CT * (c - CHUNKS))
                turn_tiles(bank, src, at).then_inc(x1t_done, 1)

            ROUTER = slice(4 * P, 4 * P + EXPERTS)

            def router(bank, b):
                for k in range(BT):
                    tok = slice((b * BT + k) * P, (b * BT + k + 1) * P)
                    ins = three(bank[:, k * EXPERTS:(k + 1) * EXPERTS], x1T_hi[:, tok], x1T_lo[:, tok],
                                w1_hi[:, ROUTER], w1_lo[:, ROUTER])
                return ins

            turn(TILES - 2, 0)
            layer1_columns(0, X, v_lo_ready, CHUNKS + 1)
            layer1_columns(1, SH[0], exp_done, TILES - 1)
            weighted(TILES - 3, 1, 1)
            turn(TILES - 1, 1)
            weighted(TILES - 2, 0, 1)
            pe.wait_ge(x1t_lo, 2)
            pe.wait_ge(l1w_ready, 1 + 2 * EXPERTS)
            router(SH[1], 0).then_inc(router_done, 1)
            weighted(TILES - 1, 1, 1)

            def up_side(c, e):
                n, cols = EXPERTS * c + e, chunk(c)
                late = at_least(c, 1) or e >= 2
                if late:
                    pe.wait_ge(gc_ready, n - 1)
                three(SH[e % 2], gup_hi[:, e, 0, :], gup_lo[:, e, 0, :], x1T_hi[:, cols],
                      x1T_lo[:, cols]).then_inc(gate_done, 1)
                if late:
                    pe.wait_ge(ub_ready, n - 1)
                three(SH[2 + e % 2], gup_hi[:, e, 1, :], gup_lo[:, e, 1, :], x1T_hi[:, cols],
                      x1T_lo[:, cols]).then_inc(up_done, 1)

            def spread(c, e):
                n = EXPERTS * c + e
                if isinstance(c, int) and n >= 2:
                    pe.wait_ge(actw_ready, n - 1)
                mm(T[e % 2], sel16[:, e, :], wT16[:, chunk(c)], start=True, stop=True).then_inc(wb_done, 1)

            def down_side(c, e):
                n = EXPERTS * c + e
                if e == 0 and at_least(c, 1):
                    pe.wait_ge(gt_ready, c)
                pe.wait_ge(actw_ready, n + 1)
                mm(O, down_sb[:, e, :], actw[:, e % 2, :], start=(e == 0),
                   stop=(e == EXPERTS - 1)).then_inc(down_done, 1)
                if e == 0:
                    mm(O, db_hi[:, :], wT16[:, chunk(c)], start=False, stop=False)
                    mm(O, db_lo[:, :], wT16[:, chunk(c)], start=False, stop=False)

            def turn_back(c):
                pe.wait_ge(prod_ready, c + 1)
                if at_least(c, 1):
                    pe.wait_ge(x2_ready, c)
                for k in range(CT):
                    ins = nc.tensor.transpose(X[:, k * P:(k + 1) * P], prodT[:, k * P:(k + 1) * P],
                                              ident[:, :])
                ins.then_inc(turned, 1)

            def step(c, e):
                up_side(c, e)
                if exists(before(c, e, 3)[0]):
                    down_side(*before(c, e, 3))
                if exists(before(c, e, 1)[0]):
                    spread(*before(c, e, 1))

            def weight_columns(bank, b):
                for k in range(BT):
                    ins = nc.tensor.transpose(bank[0:2 * EXPERTS, :].bitcast(f16)[:, k * P:(k + 1) * P],
                                              w16[:, b * BT + k, :], ident16[:, :])
                return ins

            up_side(0, 0)
            pe.wait_ge(logits_read, 1)
            up_side(0, 1)
            pe.wait_ge(w16_ready, 1)
            weight_columns(X, 0).then_inc(wt_done, 1)
            pe.wait_ge(wt_ready, 1)
            pe.wait_ge(o_read, TILES)
            spread(0, 0)
            for e in range(2, EXPERTS):
                step(0, e)
                if e >= 4:
                    layer1_columns(e - 2, X, *((wt_ready, 1) if e == 4 else (x1t_lo, e - 2)))

            def proj(bank, i, c):
                w, cols = slice(i * P, (i + 1) * P), chunk(c)
                return three(bank, w1_hi[:, w], w1_lo[:, w], x1T_hi[:, cols], x1T_lo[:, cols])

            pe.wait_ge(gc_ready, EXPERTS)
            pe.wait_ge(ub_ready, EXPERTS)
            for n, (kind, j, s) in enumerate(USES):
                bank = RING[n % len(RING)]
                if n >= len(RING):
                    by_act, by_dve = reads_until(n - len(RING))
                    pe.wait_ge(*((use_dve, by_dve) if USES[n - len(RING)][0] in BY_DVE
                                 else (use_act, by_act)))
                elif bank is X:
                    pe.wait_ge(x1t_lo, CHUNKS + 2)
                elif bank is T1:
                    pe.wait_ge(actw_ready, EXPERTS - 2)
                if kind == "rt":
                    ins = router(bank, 1)
                elif kind == "wt":
                    pe.wait_ge(w16_ready, 2)
                    ins = weight_columns(bank, 1)
                elif kind == "dk":
                    pe.wait_ge(x1t_lo, CHUNKS + j + 1)
                    ins = proj(bank, IK, CHUNKS + j)
                elif kind == "dv":
                    ins = proj(bank, IV, CHUNKS + j)
                elif kind == "v1":
                    ins = proj(bank, IV, 2 + j)
                elif kind == "q":
                    ins = proj(bank, IQ, j + 2 * s)
                elif kind == "hs":
                    q_n = use_of("q", j, s)[0]
                    pe.wait_ge(use_dve, reads_until(q_n)[1])
                    ins = mm(bank, headsum[:, :], qk[j][:, s, :], start=True, stop=True)
                else:
                    pe.wait_ge(ctx_ready, 2 * j + s + 1)
                    ins = mm(bank, w1_sb[:, OUT * P:OUT * P + P], ctxT[j][:, s, :], start=True, stop=True)
                ins.then_inc(use_done, 1)
            by_act, by_dve = reads_until(len(USES) - 1)
            pe.wait_ge(use_act, by_act)
            pe.wait_ge(use_dve, by_dve)

            with pe.Fori(1, CHUNKS) as c:
                for e in range(EXPERTS):
                    step(c, e)
                    if e == 6:
                        turn_back(c - 1)
            spread(CHUNKS - 1, EXPERTS - 1)
            for e in range(EXPERTS - 3, EXPERTS):
                down_side(CHUNKS - 1, e)
            turn_back(CHUNKS - 1)


def kernel(**inputs):
    import numpy as np
    import concourse.bacc as bacc
    from concourse.bass_utils import run_bass_kernel_spmd

    a = {k: np.asarray(v) for k, v in inputs.items()}
    in_w = a["L1_attn_in_proj_weight"].reshape(HEADS, 3, HD, P).transpose(1, 0, 2, 3).reshape(3, P, P)
    in_b = a["L1_attn_in_proj_bias"].reshape(HEADS, 3, HD).transpose(1, 0, 2).reshape(3, P)
    gup = a["L1_ffn_gate_up_proj"].reshape(EXPERTS, P, P, 2).transpose(1, 0, 3, 2)
    gub = a["L1_ffn_gate_up_proj_bias"].reshape(EXPERTS, P, 2)
    arrays = {
        "x": a["L0_attn_x"].reshape(TOKENS, P),
        "w0": np.stack([a["L0_attn_Wq"], a["L0_attn_Wk"], a["L0_attn_Wv"].T], axis=1),
        "w1s": np.concatenate([in_w[0].T, in_w[1].T, in_w[2].T, a["L1_attn_out_proj_weight"].T,
                               a["L1_ffn_router_weight"]], axis=1),
        "vecs": np.stack([a["L0_ffn_ln_gamma"], a["L0_ffn_ln_beta"],
                          *a["L0_ffn_fc1_bias"].reshape(FB, P), in_b[0], in_b[2],
                          a["L1_attn_out_proj_bias"], *gub[:, :, 0], *gub[:, :, 1]], axis=1),
        "q1": a["L0_ffn_fc1_q"],
        "q2": a["L0_ffn_fc2_q"].reshape(FB, P, P).transpose(1, 0, 2),
        "s1": a["L0_ffn_fc1_scales"].reshape(FFN),
        "s2": a["L0_ffn_fc2_scales"],
        "b2": a["L0_ffn_fc2_bias"],
        "gup": gup,
        "down": a["L1_ffn_down_proj"].transpose(1, 0, 2),
        "db": np.concatenate([a["L1_ffn_down_proj_bias"]] * 2, axis=0),
    }
    nc = bacc.Bacc("TRN2", target_bir_lowering=False, num_devices=1)
    arrays = {k: np.ascontiguousarray(v) for k, v in arrays.items()}
    args = [nc.dram_tensor(k, v.shape, mybir.dt.from_np(v.dtype), kind="ExternalInput").ap()
            for k, v in arrays.items()]
    out = nc.dram_tensor("out", (TOKENS, P), mybir.dt.float32, kind="ExternalOutput").ap()
    build(nc, *args, out)
    r = run_bass_kernel_spmd(nc, [arrays], core_ids=[0])
    return r.results[0]["out"].reshape(BATCHES, KEYS, P)
```

```python
from contextlib import ExitStack

import concourse.bass as bass
from concourse import mybir

P = 128
TOKENS = 2048
TILES = TOKENS // P
BATCHES = 2
BT = TILES // BATCHES
KEYS = TOKENS // BATCHES
CHUNK = 512
CHUNKS = TOKENS // CHUNK
CT = CHUNK // P
FFN = 512
FB = FFN // P
EXPERTS = 8
HEADS = 16
HD = P // HEADS
EPS = 1e-5
NORM_FACT = float(P) ** -0.5
HEAD_SCALE = float(HD) ** -0.5
ZERO_POINT = 128.0
ALPHA, LIMIT = 1.702, 7.0
RSQRT_MAGIC = float(0x5F3759DF)
LOWEST = -3.0e38

GAMMA, BETA, FC1B, BQ, BV, BO, GB = 0, 1, 2, 6, 7, 8, 9
UB = GB + EXPERTS
VECS = UB + EXPERTS
WQ, WK, WVT = 0, 1, 2
IQ, IK, IV, OUT = 0, 1, 2, 3
F_ORDER = (1, 2, 3, 0)


BESIDE = 8


def build(nc, x, w0, w1s, vecs, q1, q2, s1, s2, b2, gup, down, db, out):
    f32, f16, i32 = mybir.dt.float32, mybir.dt.float16, mybir.dt.int32
    ALU = mybir.AluOpType
    ACT = mybir.ActivationFunctionType
    AX = mybir.AxisListType
    ds = bass.ds

    x_rows = x.rearrange("(t p) d -> p t d", p=P)
    out_rows = out.rearrange("(t p) d -> p t d", p=P)

    ctx = ExitStack()
    with ctx:
        def sb(name, shape, dt=f32):
            return ctx.enter_context(nc.sbuf_tensor(name, shape, dt))

        def sem(name):
            return ctx.enter_context(nc.semaphore(name))

        ident = sb("ident", [P, P])
        ident16 = sb("ident16", [P, P], f16)
        headsum = sb("headsum", [P, P])
        sel16 = sb("sel16", [2 * EXPERTS, EXPERTS, P], f16)
        rank = sb("rank", [P, EXPERTS])
        scratch = sb("scratch", [P, 1])
        scratch_dve = sb("scratch_dve", [P, 3])

        x_sb = sb("x_sb", [P, TILES, P])
        xn = sb("xn", [P, TILES, P])
        hz = sb("hz", [P, TILES, P])
        xnb = sb("xnb", [P, TILES, P])
        gate0 = sb("gate0", [P, TILES, P])
        xT_hi = sb("xT_hi", [P, TOKENS], f16)
        xT_lo = sb("xT_lo", [P, TOKENS], f16)
        hT32 = sb("hT32", [P, 2, CHUNK])
        hT_hi = sb("hT_hi", [P, TOKENS], f16)
        hT_lo = sb("hT_lo", [P, TOKENS], f16)
        kT_hi = sb("kT_hi", [P, TOKENS], f16)
        kT_lo = sb("kT_lo", [P, TOKENS], f16)
        v_hi = sb("v_hi", [P, TILES, P], f16)
        v_lo = sb("v_lo", [P, TILES, P], f16)
        yT = sb("yT", [P, FB, CHUNK])
        u0 = sb("u0", [P, CHUNK])
        probs = sb("probs", [P, 2, KEYS])
        pT_hi = sb("pT_hi", [P, 2, KEYS], f16)
        pT_lo = sb("pT_lo", [P, 2, KEYS], f16)
        sg0 = sb("sg0", [P, 2, P])
        x1 = hz

        stats = sb("stats", [P, TILES, 6])
        mv = sb("mv", [P, TILES, 2])
        stats1 = sb("stats1", [P, TILES, 6])
        mv1 = sb("mv1", [P, TILES, 2])
        rs_arg = sb("rs_arg", [P, 2, TILES])
        rs = sb("rs", [P, 2, TILES])
        rs1_arg = sb("rs1_arg", [P, TILES])
        rs1 = sb("rs1", [P, TILES])
        x1_bias = sb("x1_bias", [P, TILES])
        hz_bias = sb("hz_bias", [P, TILES])
        half_a = sb("half_a", [P, 2, TILES])
        seed = sb("seed", [P, 2, TILES], i32)
        newt = sb("newt", [P, 2, TILES])
        newt2 = sb("newt2", [P, 2, TILES])
        neg_max = sb("neg_max", [P, TILES])
        row_sum = sb("row_sum", [P, TILES])
        row_inv = sb("row_inv", [P, TILES])

        w0_sb = sb("w0_sb", [P, 3, P])
        A_hi = sb("A_hi", [P, P], f16)
        A_lo = sb("A_lo", [P, P], f16)
        wv_hi = sb("wv_hi", [P, P], f16)
        wv_lo = sb("wv_lo", [P, P], f16)
        vecs_sb = sb("vecs_sb", [P, VECS])
        ub1 = sb("ub1", [P, EXPERTS])
        bo_half = sb("bo_half", [P, 1])
        q1_sb = sb("q1_sb", [P, FFN], i32)
        q2_sb = sb("q2_sb", [P, FB, P], i32)
        s1_sb = sb("s1_sb", [P, FFN])
        s2_sb = sb("s2_sb", [P, FB, P])
        b2_sb = sb("b2_sb", [P, P])
        fc1_w = sb("fc1_w", [P, FFN])
        th3 = fc1_w
        fc1_hi = sb("fc1_hi", [P, FFN], f16)
        fc1_lo = sb("fc1_lo", [P, FFN], f16)
        fc2_w = sb("fc2_w", [P, FB, P])

        W1COLS = 4 * P + EXPERTS
        w1_sb = sb("w1_sb", [P, W1COLS])
        w1_hi = sb("w1_hi", [P, W1COLS], f16)
        w1_lo = sb("w1_lo", [P, W1COLS], f16)
        wneg_hi = sb("wneg_hi", [P, 2 * P], f16)
        wneg_lo = sb("wneg_lo", [P, 2 * P], f16)
        gup_sb = sb("gup_sb", [P, EXPERTS, 2, P])
        gup_hi = sb("gup_hi", [P, EXPERTS, 2, P], f16)
        gup_lo = sb("gup_lo", [P, EXPERTS, 2, P], f16)
        down_sb = sb("down_sb", [P, EXPERTS, P])
        db_sb = sb("db_sb", [2 * EXPERTS, P])
        db_hi = sb("db_hi", [2 * EXPERTS, P], f16)
        db_lo = sb("db_lo", [2 * EXPERTS, P], f16)

        x1n = xn
        x1T_hi = sb("x1T_hi", [P, TOKENS], f16)
        x1T_lo = sb("x1T_lo", [P, TOKENS], f16)
        sT = xnb[:, :, :].rearrange("p t d -> p (t d)")

        dkT, dvT = (probs[:, k, :].rearrange("p (j n) -> p j n", j=2) for k in range(2))
        v1T = hT_hi[:, :].bitcast(f32).rearrange("p (j n) -> p j n", j=2)

        def quad(*halves):
            return [h.bitcast(f32).rearrange("p (s n) -> p s n", s=2) for h in halves]

        qk = quad(kT_hi[:, :], kT_lo[:, :])
        qk_hi, qk_lo = (sb(name, [P, 2, 2, CHUNK], f16) for name in ("qk_hi", "qk_lo"))
        headsum16 = sb("headsum16", [P, P], f16)
        th = quad(*(v[:, :, :].rearrange("p t d -> p (t d)") for v in (v_hi, v_lo)))
        adv = quad(*(v[:, :, :].rearrange("p t d -> p (t d)") for v in (pT_hi, pT_lo)))
        ctxT = quad(xT_hi[:, :], xT_lo[:, :])

        BE = [P, BT, EXPERTS]
        logits, logits2, equal, ranked, first, second, wrow = (
            sb(name, BE) for name in ("logits", "logits2", "equal", "ranked", "first", "second", "wrow"))
        top1, top2, best, gap, e_gap, wden, wtop1, wtop2 = (
            sb(name, [P, BT]) for name in ("top1", "top2", "best", "gap", "e_gap", "wden", "wtop1", "wtop2"))
        w16 = sb("w16", [P, TILES, 2 * EXPERTS], f16)
        wT16 = sb("wT16", [2 * EXPERTS, TOKENS], f16)
        halved = sb("halved", [EXPERTS, TOKENS])
        halved_dram = nc.dram_tensor("halved_dram", (CHUNKS * EXPERTS, CHUNK), f32, kind="Internal").ap()

        def pair(big, k):
            return big[:, k * 2 * CT:(k + 1) * 2 * CT, :].rearrange("p (j t) d -> p j (t d)", j=2)

        wb_slots = [pair(big, 1)[:, j, :] for big in (gate0, x_sb) for j in range(2)]
        SLOTS = len(wb_slots)
        BY_DRAM = (1, EXPERTS - 2)
        g_c, g_s = pair(gate0, 0), sb("g_s", [P, 2, CHUNK])
        u_b, u_c = pair(x_sb, 0), sb("u_c", [P, 2, CHUNK])
        glu, act32, actw = yT[:, 0:2, :], yT[:, 2:4, :], hT32
        o_sum = sb("o_sum", [P, CHUNK])
        o_th = sb("o_th", [P, CHUNK])
        gT = sb("gT", [P, CHUNK])
        prodT = sb("prodT", [P, CHUNK])

        S = [ctx.enter_context(nc.psum_tensor(f"S{i}", [P, 2 * CHUNK], f32)) for i in range(2)]
        T0, T1, O, X = (ctx.enter_context(nc.psum_tensor(n, [P, CHUNK], f32))[:, :]
                        for n in ("T0", "T1", "O", "X"))
        T = (T0, T1)
        SH = [S[0][:, 0:CHUNK], S[0][:, CHUNK:2 * CHUNK], S[1][:, 0:CHUNK], S[1][:, CHUNK:2 * CHUNK]]

        FC2_BANK = [SH[0]] * (CHUNKS - 1) + [X]

        USES = (
            (0, 3, "start", "columns", 2, 0), (0, 4, "middle", "dk", 0, 0),
            (0, 5, "start", "q", 0, 0), (0, 5, "middle", "v1", 0, 0),
            (0, 6, "start", "q", 0, 1), (0, 6, "middle", "dv", 0, 0),
            (0, 7, "start", "columns", 3, 0), (0, 7, "middle", "headsum", 0, 0),
            (1, 0, "start", "dk", 1, 0), (1, 0, "middle", "router", 0, 0),
            (1, 1, "start", "q", 1, 0), (1, 1, "middle", "headsum", 0, 1),
            (1, 2, "start", "q", 1, 1), (1, 2, "middle", "out", 0, 0),
            (1, 3, "start", "v1", 1, 0), (1, 3, "middle", "dv", 1, 0),
            (1, 4, "start", "headsum", 1, 0), (1, 4, "middle", "headsum", 1, 1),
            (1, 5, "start", "halved", 0, 1), (1, 5, "middle", "out", 0, 1),
            (1, 6, "start", "out", 1, 0), (1, 6, "middle", "weights", 0, 0),
            (1, 7, "start", "halved", 0, 2), (1, 7, "middle", "rows", 0, 0),
            (CHUNKS, 0, "start", "out", 1, 1))
        ADV_AT = {(1, 0): ((0, 0),), (1, 2): ((0, 1),), (1, 4): ((1, 0),), (1, 5): ((1, 1),)}
        SPLIT_AT = {(0, 6): ((0, 0),), (0, 7): ((0, 1),), (1, 2): ((1, 0),), (1, 3): ((1, 1),)}
        CTX_AT = {(1, 1): ((0, 0),), (1, 3): ((0, 1),), (1, 5): ((1, 0),), (1, 6): ((1, 1),)}
        MIDDLE_FIRST = ((0, 7), (1, 1), (1, 4), (1, 5), (1, 6))
        SPLIT_ORDER = [u for at in SPLIT_AT.values() for u in at]
        ADV_ORDER, CTX_ORDER = ([u for at in table.values() for u in at]
                                for table in (ADV_AT, CTX_AT))
        GROUPS = ((0, BT), (BT, BT + CT), (BT + CT, TILES))
        BY_DVE = ("router", "q")


        def uses_at(c, e, place):
            if not isinstance(c, int):
                return []
            return [(n, *u[3:]) for n, u in enumerate(USES) if u[:3] == (c, e, place)]

        def use_count(n):
            return sum(reads_until(n))

        def at(table, c, e):
            return table.get((c, e), ()) if isinstance(c, int) else ()

        def bank_of_out(c):
            return T0 if c == CHUNKS else X

        def use_of(kind, j=0, s=0):
            return [u[3:] for u in USES].index((kind, j, s))

        def reads_until(n):
            kinds = [u[3] for u in USES[:n + 1] if u[3] not in ("columns", "rows")]
            dve = sum(k in BY_DVE for k in kinds)
            return len(kinds) - dve, dve

        def wait_read(engine, n):
            kind, j = USES[n][3:5]
            by_act, by_dve = reads_until(n)
            engine.wait_ge(*((x1t_lo, j + 1) if kind == "columns" else (x2_ready, 1) if kind == "rows" else
                             (use_dve, by_dve) if kind in BY_DVE else (use_act, by_act)))

        x_in = [sem(f"x_in{c}") for c in range(CHUNKS)]
        wb_in = [sem(f"wb_in{k}") for k in range(SLOTS)]
        out_done = sem("out_done")
        dve_self, pool_self = sem("dve_self"), sem("pool_self")
        (w0_in, vecs_in, ffn1_in, ffn2_in, l1_in, stats0_ready, consts_ready, fc1_ready, fc1_hi_ready, fc1_lo_ready,
         fc2_ready, wv_hi_ready, wv_ready, A_ready, A_hi_ready, A_lo_ready, scales_ready, xn_ready, hz_ready,
         xt_done, ht_done, xt_hi_ready, xt_lo_ready, h32_ready, h_hi_ready, h_lo_ready, xnb_ready,
         fc1_done, y_ready, fc2_done, u_ready, gate0_ready, th3_ready, gate3_ready, k_done, k_hi_ready, k_lo_ready,
         v_done, v_hi_ready, v_lo_ready, s_done, max_ready, exp_done, pt_done, pt_hi_ready,
         pt_lo_ready, o_done, o_read, x1_ready, stats_ready, seed_ready, rs1_ready, x1n_pool, x1n_act, l1w_ready,
         x1t_done, x1t_hi, x1t_lo, router_done, logits_read, gap_ready, egap_ready, w16_ready,
         wt_done, wt_ready, halved_done, halved_last, halved_out,
         use_done, use_act, use_dve, qk_hi_ready, qk_lo_ready, adv_ready, ctx_ready,
         gate_done, up_done, wb_done, down_done, gb_ready, gc_ready, gs_ready, ub_ready, uc_ready, glu_ready,
         act_ready, last_act_ready, actw_ready, sum_read, oth_ready, gt_ready, prod_ready, turned, x2_ready) = (
            sem(n) for n in (
                "w0_in vecs_in ffn1_in ffn2_in l1_in stats0_ready consts_ready fc1_ready fc1_hi_ready fc1_lo_ready "
                "fc2_ready wv_hi_ready wv_ready A_ready A_hi_ready A_lo_ready scales_ready xn_ready hz_ready "
                "xt_done ht_done xt_hi_ready xt_lo_ready h32_ready h_hi_ready h_lo_ready xnb_ready "
                "fc1_done y_ready+ fc2_done u_ready gate0_ready+ th3_ready gate3_ready k_done k_hi_ready k_lo_ready+ "
                "v_done v_hi_ready v_lo_ready+ s_done max_ready exp_done pt_done pt_hi_ready "
                "pt_lo_ready o_done o_read x1_ready stats_ready seed_ready rs1_ready x1n_pool x1n_act l1w_ready "
                "x1t_done x1t_hi x1t_lo router_done logits_read gap_ready egap_ready w16_ready "
                "wt_done wt_ready halved_done halved_last halved_out "
                "use_done use_act use_dve qk_hi_ready qk_lo_ready adv_ready ctx_ready "
                "gate_done up_done wb_done down_done gb_ready gc_ready gs_ready ub_ready uc_ready glu_ready "
                "act_ready last_act_ready actw_ready sum_read oth_ready gt_ready prod_ready turned x2_ready").split())

        block = ctx.enter_context(nc.Block())

        def bc(ap, n):
            return ap.unsqueeze(2).broadcast_to([P, ap.shape[1], n])

        def tiles_of(bank):
            return bank.rearrange("p (t d) -> p t d", d=P)

        def chunk(c):
            return ds(c * CHUNK, CHUNK)

        HALVES = (slice(0, CHUNK // 2), slice(CHUNK // 2, CHUNK))

        def half_tiles(n):
            return slice(TILES - CT + n * CT // 2, TILES - CT + (n + 1) * CT // 2)

        def before(c, e, lag):
            return (c, e - lag) if e >= lag else (c - 1, e - lag + EXPERTS)

        def exists(c):
            return not isinstance(c, int) or c >= 0

        def at_least(c, k):
            return c >= k if isinstance(c, int) else True

        def by_dram(c, e):
            return not isinstance(c, int) or (c, e) >= BY_DRAM

        def spread_of(c, e):
            return wb_slots[e % SLOTS] if by_dram(c, e) else T[e % 2]

        @block.sync
        def _(sp):
            for c in range(CHUNKS):
                sp.dma_start(x_sb[:, c * CT:(c + 1) * CT, :],
                             x_rows[:, c * CT:(c + 1) * CT, :]).then_inc(x_in[c], 16)
            for dst, src in ((q2_sb[:, :, :], q2), (s2_sb[:, :, :], s2.partition_broadcast(P)),
                             (b2_sb[:, :], b2.partition_broadcast(P))):
                sp.dma_start(dst, src).then_inc(ffn2_in, 16)
            sp.wait_ge(xn_ready, 1)
            for dst, src in ((w1_sb[:, :], w1s), (gup_sb[:, :, :, :], gup),
                             (down_sb[:, :, :], down), (db_sb[:, :], db)):
                sp.dma_start(dst, src).then_inc(l1_in, 16)

            def store_halved(c):
                sp.dma_start(halved_dram[c * EXPERTS:(c + 1) * EXPERTS, :],
                             halved[:, chunk(c)]).then_inc(halved_out, 16)

            def spread_weights(c, e):
                n = EXPERTS * c + e
                sp.wait_ge(actw_ready, n + 1 - SLOTS)
                sp.dma_start(wb_slots[e % SLOTS].unsqueeze(1),
                             halved_dram[ds(n, 1), :].partition_broadcast(P)).then_inc(wb_in[e % SLOTS], 16)

            def store_rows(c):
                sp.wait_ge(x2_ready, c + 1)
                sp.dma_start(out_rows[:, ds(c * CT, CT), :],
                             x1[:, ds(c * CT, CT), :]).then_inc(out_done, 16)

            sp.wait_ge(use_act, reads_until(use_of("halved", 0, 1))[0])
            store_halved(1)
            sp.wait_ge(x1_ready, TILES)
            sp.wait_ge(halved_out, 16)
            for e in range(BY_DRAM[1], EXPERTS):
                spread_weights(1, e)
            sp.wait_ge(use_act, reads_until(use_of("halved", 0, 2))[0])
            store_halved(2)
            sp.wait_ge(halved_last, 1)
            store_halved(CHUNKS - 1)
            sp.wait_ge(halved_out, 16 * 3)
            with sp.Fori(2, CHUNKS) as c:
                for e in range(EXPERTS):
                    spread_weights(c, e)
                store_rows(c - 2)
            store_rows(CHUNKS - 2)
            for n in range(2):
                sp.wait_ge(x2_ready, CHUNKS + n)
                sp.dma_start(out_rows[:, half_tiles(n), :], x1[:, half_tiles(n), :]).then_inc(out_done, 16)
            sp.wait_ge(out_done, 16 * (CHUNKS + 1))

        @block.gpsimd
        def _(pool):
            g = nc.gpsimd
            n_self = [0]

            def link(ins):
                n_self[0] += 1
                ins.then_inc(pool_self, 1)
                pool.wait_ge(pool_self, n_self[0])

            def diagonal(ap, base, pattern, fill=1.0):
                return g.affine_select(out=ap, in_=ap, compare_op=ALU.not_equal, fill=fill,
                                       base=base, pattern=pattern, channel_multiplier=1)

            link(g.memset(ident[:, :], 0.0))
            diagonal(ident[:, :], 0, [[-1, P]]).then_inc(consts_ready, 1)

            pool.wait_ge(wv_hi_ready, 1)
            g.tensor_tensor(wv_lo[:, :], w0_sb[:, WVT, :], wv_hi[:, :],
                            ALU.subtract).then_inc(wv_ready, 1)
            pool.wait_ge(ffn2_in, 16 * 3)
            g.tensor_scalar(fc2_w[:, :, :], q2_sb[:, :, :], -ZERO_POINT, None, ALU.add)\
                .then_inc(fc2_ready, 1)
            pool.wait_ge(fc1_hi_ready, 1)
            g.tensor_tensor(fc1_lo[:, :], fc1_w[:, :], fc1_hi[:, :],
                            ALU.subtract).then_inc(fc1_lo_ready, 1)

            def h_lo(c):
                pool.wait_ge(h_hi_ready, c + 1)
                g.tensor_tensor(hT_lo[:, chunk(c)], hT32[:, c % 2, :], hT_hi[:, chunk(c)],
                                ALU.subtract).then_inc(h_lo_ready, 1)

            def residual_of_ffn(c):
                pool.wait_ge(xn_ready, CT * (c + 1))
                g.tensor_tensor(xnb[:, c * CT:(c + 1) * CT, :], xn[:, c * CT:(c + 1) * CT, :],
                                b2_sb[:, :].unsqueeze(1).broadcast_to([P, CT, P]),
                                ALU.add).then_inc(xnb_ready, 1)

            h_lo(0)
            pool.wait_ge(fc2_ready, 1)
            g.tensor_tensor(fc2_w[:, :, :], fc2_w[:, :, :], s2_sb[:, :, :],
                            ALU.mult).then_inc(fc2_ready, 1)
            link(g.tensor_scalar(b2_sb[:, :], b2_sb[:, :], 0.5, None, ALU.mult))
            residual_of_ffn(0)
            for c in range(1, CHUNKS):
                h_lo(c)
                residual_of_ffn(c)

            g.memset(ident16[:, :], 0.0)
            g.memset(headsum[:, :], 1.0)
            for e in range(EXPERTS):
                g.memset(rank[:, e:e + 1], float(EXPERTS - e))
            link(g.memset(sel16[:, :, :], 0.0))
            diagonal(ident16[:, :], 0, [[-1, P]])
            link(diagonal(sel16[:, :, :], 0, [[-1, EXPERTS], [0, P]], 0.5))
            diagonal(sel16[:, :, :], -EXPERTS, [[-1, EXPERTS], [0, P]], 0.5)
            hs = headsum[:, :].rearrange("p (h d) -> p h d", d=HD)
            link(g.affine_select(out=hs, in_=hs, compare_op=ALU.is_ge, fill=0.0, base=0,
                                 pattern=[[-HD, HEADS], [0, HD]], channel_multiplier=1))
            link(g.affine_select(out=hs, in_=hs, compare_op=ALU.is_ge, fill=0.0, base=HD - 1,
                                 pattern=[[HD, HEADS], [0, HD]], channel_multiplier=-1))
            pool.wait_ge(l1_in, 16 * 4)
            g.tensor_copy(headsum16[:, :], headsum[:, :])
            g.tensor_scalar(ub1[:, :], vecs_sb[:, UB:UB + EXPERTS], 1.0, None, ALU.add)
            g.tensor_scalar(bo_half[:, :], vecs_sb[:, BO:BO + 1], 0.5, None, ALU.mult)
            g.tensor_copy(db_hi[:, :], db_sb[:, :])
            link(g.tensor_copy(w1_hi[:, :], w1_sb[:, :]))
            link(g.tensor_tensor(w1_lo[:, :], w1_sb[:, :], w1_hi[:, :], ALU.subtract))
            for neg, w in ((wneg_hi, w1_hi), (wneg_lo, w1_lo)):
                g.tensor_scalar(neg[:, :], w[:, IK * P:(IV + 1) * P], -1.0, None, ALU.mult)
            g.tensor_tensor(db_lo[:, :], db_sb[:, :], db_hi[:, :], ALU.subtract).then_inc(l1w_ready, 1)

            pool.wait_ge(th3_ready, 1)
            link(g.tensor_scalar(th3[:, :], th3[:, :], 0.5, 0.5, ALU.mult, ALU.add))
            g.tensor_tensor(gate0[:, TILES - CT:TILES, :], tiles_of(u0[:, :]), tiles_of(th3[:, :]),
                            ALU.mult).then_inc(gate3_ready, 1)

            def residual(t, j):
                pool.wait_ge(o_read, t + 1)
                g.tensor_tensor(x1[:, ds(t, 1), :], sg0[:, j:j + 1, :], x_sb[:, ds(t, 1), :],
                                ALU.add).then_inc(x1_ready, 1)

            with pool.Fori(0, BT // 2) as half:
                for j in range(2):
                    t = 2 * half + j
                    g.tensor_copy(gup_hi[:, ds(t, 1), :, :], gup_sb[:, ds(t, 1), :, :])\
                        .then_inc(l1w_ready, 1)
                    pool.wait_ge(l1w_ready, 2 * t + 2)
                    g.tensor_tensor(gup_lo[:, ds(t, 1), :, :], gup_sb[:, ds(t, 1), :, :],
                                    gup_hi[:, ds(t, 1), :, :], ALU.subtract).then_inc(l1w_ready, 1)
                    residual(t, j)

            def newton(b):
                r = slice(*GROUPS[b])
                pool.wait_ge(seed_ready, b + 1)
                src = seed[:, 0, r].bitcast(f32)
                for k in range(3):
                    if (b, k) == (0, 2):
                        residual(BT + 1, 1)
                    link(g.tensor_tensor(newt[:, 0, r], src, src, ALU.mult))
                    link(g.tensor_tensor(newt2[:, 0, r], newt[:, 0, r], half_a[:, 0, r], ALU.mult))
                    link(g.tensor_scalar(newt[:, 0, r], newt2[:, 0, r], 1.5, None, ALU.add))
                    link(g.tensor_tensor(rs1[:, r], newt[:, 0, r], src, ALU.mult))
                    src = rs1[:, r]
                link(g.tensor_tensor(newt[:, 0, r], mv1[:, r, 0], rs1[:, r], ALU.mult))
                g.tensor_scalar(x1_bias[:, r], newt[:, 0, r], -1.0, None, ALU.mult).then_inc(rs1_ready, 1)

            def norm(t0, t1):
                for t in range(t0, t1):
                    g.tensor_scalar(x1n[:, t, :], x1[:, t, :], mv1[:, t, 0:1], rs1[:, t:t + 1],
                                    ALU.subtract, ALU.mult).then_inc(x1n_pool, 1)

            residual(BT, 0)
            newton(0)
            norm(0, 2)
            residual(BT + 2, 0)
            norm(CT, CT + 2)
            for t in range(BT + 3, TILES - 1):
                residual(t, t % 2)
                if t == TILES - 3:
                    newton(1)
                elif t == TILES - 2:
                    norm(BT, BT + 2)

            def product(c, e):
                n = EXPERTS * c + e
                pool.wait_ge(glu_ready, n + 1)
                if at_least(c, 1) or e >= 2:
                    pool.wait_ge(actw_ready, n - 1)
                g.tensor_tensor(act32[:, e % 2, :], u_c[:, e % 2, :], glu[:, e % 2, :],
                                ALU.mult).then_inc(act_ready, 1)

            def gate_rows(c):
                pool.wait_ge(gt_ready, c + 1)
                if at_least(c, 1):
                    pool.wait_ge(turned, c)
                g.tensor_tensor(prodT[:, :], gT[:, :], sT[:, chunk(c)], ALU.mult).then_inc(prod_ready, 1)

            def context(j, s):
                pool.wait_ge(adv_ready, ADV_ORDER.index((j, s)) + 1)
                pool.wait_ge(use_act, reads_until(use_of("v1", j))[0])
                g.tensor_tensor(ctxT[j][:, s, :], adv[j][:, s, :], v1T[:, j, :],
                                ALU.add).then_inc(ctx_ready, 1)

            def step(c, e):
                for j, s in at(CTX_AT, c, e):
                    context(j, s)
                if exists(before(c, e, 1)[0]):
                    product(*before(c, e, 1))
                for j, s in at(SPLIT_AT, c, e):
                    pool.wait_ge(qk_hi_ready, SPLIT_ORDER.index((j, s)) + 1)
                    g.tensor_tensor(qk_lo[:, j, s, :], qk[j][:, s, :], qk_hi[:, j, s, :],
                                    ALU.subtract).then_inc(qk_lo_ready, 1)

            for e in range(EXPERTS):
                step(0, e)
                if e == 1:
                    residual(TILES - 1, 1)
                elif e == 3:
                    newton(2)
                elif e == 4:
                    norm(BT + CT, BT + CT + 2)
            for e in range(EXPERTS):
                if e == 4:
                    pool.wait_ge(use_act, reads_until(use_of("out", 0, 0))[0])
                    gate_rows(0)
                step(1, e)
            with pool.Fori(2, CHUNKS) as c:
                for e in range(EXPERTS):
                    if e == 4:
                        gate_rows(c - 1)
                    step(c, e)

        @block.scalar
        def _(act):
            a = nc.scalar
            act.dma_start(w0_sb[:, :, :], w0).then_inc(w0_in, 16)
            act.dma_start(vecs_sb[:, :], vecs).then_inc(vecs_in, 16)
            for dst, src in ((q1_sb[:, :], q1), (s1_sb[:, :], s1.partition_broadcast(P))):
                act.dma_start(dst, src).then_inc(ffn1_in, 16)

            act.wait_ge(vecs_in, 16)
            a.activation(scratch[:, :], vecs_sb[:, 0:1], ACT.Silu).then_inc(y_ready, FB)
            act.wait_ge(A_ready, 1)
            a.copy(A_hi[:, :], SH[0][:, 0:P]).then_inc(A_hi_ready, 1)
            a.copy(wv_hi[:, :], w0_sb[:, WVT, :]).then_inc(wv_hi_ready, 1)

            def second_norm(c):
                act.wait_ge(scales_ready, 1 if c == 0 else 3)
                for t in range(c * CT, (c + 1) * CT):
                    ins = a.activation(hz[:, t, :], x_sb[:, t, :], ACT.Identity,
                                       bias=hz_bias[:, t:t + 1], scale=rs[:, 1, t:t + 1])
                ins.then_inc(hz_ready, 1)

            def x_columns(c):
                act.wait_ge(xt_done, c + 1)
                a.copy(xT_hi[:, chunk(c)], T0).then_inc(xt_hi_ready, 1)

            def h_columns(c):
                act.wait_ge(ht_done, c + 1)
                if c >= 2:
                    act.wait_ge(h_lo_ready, c - 1)
                a.activation(hT32[:, c % 2, :], T1, ACT.Identity, bias=vecs_sb[:, BETA:BETA + 1],
                             scale=vecs_sb[:, GAMMA:GAMMA + 1]).then_inc(h32_ready, 1)

            def k_hi(c):
                act.wait_ge(k_done, c + 1)
                a.copy(kT_hi[:, chunk(c)], O).then_inc(k_hi_ready, 1)

            def values_hi(c):
                act.wait_ge(v_done, c + 1)
                a.activation(v_hi[:, ds(c * CT, CT), :], tiles_of(X), ACT.Copy,
                             scale=NORM_FACT).then_inc(v_hi_ready, 1)

            second_norm(0)
            x_columns(0)
            act.wait_ge(fc1_ready, 1)
            a.copy(fc1_hi[:, :], fc1_w[:, :]).then_inc(fc1_hi_ready, 1)
            h_columns(0)
            k_hi(0)
            values_hi(0)

            for c in range(CHUNKS):
                for i, f in enumerate(F_ORDER):
                    act.wait_ge(fc1_done, FB * c + i + 1)
                    a.activation(yT[:, f, :], SH[f], ACT.Silu,
                                 bias=vecs_sb[:, FC1B + f:FC1B + f + 1]).then_inc(y_ready, 1)
                if c:
                    act.wait_ge(u_ready, c)
                    a.activation(gate0[:, ds((c - 1) * CT, CT), :], tiles_of(u0[:, :]),
                                 ACT.Silu).then_inc(gate0_ready, 1)
                if c + 1 == CHUNKS:
                    break
                x_columns(c + 1)
                h_columns(c + 1)
                if c + 2 == 3:
                    second_norm(3)
                k_hi(c + 1)
                values_hi(c + 1)

            def exp(t, j):
                act.wait_ge(max_ready, t + 1)
                a.activation(probs[:, j, :], S[1 - j][:, :], ACT.Exp, bias=neg_max[:, ds(t, 1)],
                             accum_out=row_sum[:, ds(t, 1)]).then_inc(exp_done, 1)

            def split_hi(t, j):
                for h in range(2):
                    act.wait_ge(pt_done, 2 * t + h + 1)
                    a.copy(pT_hi[:, j, h * CHUNK:(h + 1) * CHUNK], T[h]).then_inc(pt_hi_ready, 1)

            def layer1_columns(c):
                act.wait_ge(x1t_done, c + 1)
                a.copy(x1T_hi[:, chunk(c)], X).then_inc(x1t_hi, 1)

            def gap_exp(b):
                act.wait_ge(gap_ready, b + 1)
                a.activation(e_gap[:, :], gap[:, :], ACT.Exp).then_inc(egap_ready, 1)

            def norm(b, t0, t1):
                act.wait_ge(rs1_ready, b + 1)
                for t in range(t0, t1):
                    a.activation(x1n[:, t, :], x1[:, t, :], ACT.Identity, bias=x1_bias[:, t:t + 1],
                                 scale=rs1[:, t:t + 1]).then_inc(x1n_act, 1)

            exp(0, 0)
            exp(1, 1)
            split_hi(0, 0)
            act.wait_ge(u_ready, CHUNKS)
            a.activation(th3[:, :], u0[:, :], ACT.Tanh, scale=0.5).then_inc(th3_ready, 1)
            split_hi(1, 1)
            exp(2, 0)
            with act.Fori(1, (BT + 2) // 2) as half:
                for j in range(2):
                    split_hi(2 * half + j, j)
                    exp(2 * half + j + 1, 1 - j)
            for t in range(BT + 2, TILES):
                split_hi(t, t % 2)
                if t + 1 < TILES:
                    exp(t + 1, 1 - t % 2)
                if t in (BT + 3, BT + 4):
                    norm(0, CT * (t - BT - 3) + 2, CT * (t - BT - 2))
                if t in (BT + 4, BT + 5):
                    layer1_columns(t - BT - 4)

            def gate_bias(c, e):
                n = EXPERTS * c + e
                act.wait_ge(gate_done, n + 1)
                if at_least(c, 1) or e >= 2:
                    act.wait_ge(glu_ready, n - 1)
                a.activation(g_c[:, e % 2, :], SH[e % 2], ACT.Identity,
                             bias=vecs_sb[:, GB + e:GB + e + 1]).then_inc(gb_ready, 1)

            def gate_tanh(c, e):
                n = EXPERTS * c + e
                act.wait_ge(gc_ready, n + 1)
                if at_least(c, 1) or e >= 2:
                    act.wait_ge(glu_ready, n - 1)
                a.activation(g_s[:, e % 2, :], g_c[:, e % 2, :], ACT.Tanh,
                             scale=0.5 * ALPHA).then_inc(gs_ready, 1)

            def up_bias(c, e):
                n = EXPERTS * c + e
                act.wait_ge(up_done, n + 1)
                if at_least(c, 1) or e >= 2:
                    act.wait_ge(uc_ready, n - 1)
                a.activation(u_b[:, e % 2, :], SH[2 + e % 2], ACT.Identity,
                             bias=ub1[:, e:e + 1]).then_inc(ub_ready, 1)

            def finish(c):
                act.wait_ge(down_done, EXPERTS * (c + 1))
                if at_least(c, 1):
                    act.wait_ge(gt_ready, c)
                a.copy(o_sum[:, :], O).then_inc(sum_read, 1)
                act.wait_ge(sum_read, c + 1)
                a.activation(o_th[:, :], o_sum[:, :], ACT.Tanh, scale=0.5).then_inc(oth_ready, 1)

            def pair_attention(c, e, place):
                for n, kind, j, s in uses_at(c, e, place):
                    if kind == "columns":
                        layer1_columns(j)
                    if kind in BY_DVE or kind in ("columns", "rows"):
                        continue
                    act.wait_ge(use_done, use_count(n))
                    if kind == "dk":
                        ins = a.copy(dkT[:, j, :], X)
                    elif kind == "dv":
                        ins = a.activation(dvT[:, j, :], X, ACT.Copy, scale=0.5)
                    elif kind == "v1":
                        ins = a.activation(v1T[:, j, :], X, ACT.Identity, bias=vecs_sb[:, BV:BV + 1])
                    elif kind == "weights":
                        ins = a.copy(wT16[:, KEYS:2 * KEYS], X[0:2 * EXPERTS, :].bitcast(f16))
                    elif kind == "halved":
                        ins = a.copy(halved[:, chunk(s)], X[0:EXPERTS, :])
                    elif kind == "headsum":
                        ins = a.activation(th[j][:, s, :], X, ACT.Tanh, scale=0.5 * HEAD_SCALE)
                    else:
                        ins = a.activation(sT[:, chunk(j + 2 * s)], bank_of_out(c), ACT.Identity,
                                           bias=bo_half[:, :], scale=0.5)
                    ins.then_inc(use_act, 1)

            def step(c, e, beside=None):
                pair_attention(c, e, "start")
                if beside:
                    beside()
                middle_first = isinstance(c, int) and (c, e) in MIDDLE_FIRST
                gate_bias(c, e)
                if exists(before(c, e, 1)[0]) and not at_least(c, 2):
                    gate_tanh(*before(c, e, 1))
                if not middle_first:
                    up_bias(c, e)
                if at_least(c, 2):
                    gate_tanh(c, e)
                pair_attention(c, e, "middle")
                if middle_first:
                    up_bias(c, e)
                for j, s in at(SPLIT_AT, c, e):
                    act.wait_ge(use_dve, reads_until(use_of("q", j, s))[1])
                    a.copy(qk_hi[:, j, s, :], qk[j][:, s, :]).then_inc(qk_hi_ready, 1)
                if at_least(c, 1) and e == 2:
                    finish(c - 1)

            gate_bias(0, 0)
            gap_exp(0)
            up_bias(0, 0)
            norm(1, BT + 2, BT + CT)
            for e in range(1, EXPERTS):
                step(0, e)
                if e == 5:
                    norm(2, BT + CT + 2, TILES)
            for e in range(EXPERTS):
                step(1, e, beside=(lambda: gap_exp(1)) if e == 4 else None)
            gate_tanh(1, EXPERTS - 1)
            act.wait_ge(halved_done, 1)
            a.copy(halved[:, chunk(CHUNKS - 1)], T0[0:EXPERTS, :]).then_inc(halved_last, 1)
            with act.Fori(2, CHUNKS) as c:
                for e in range(EXPERTS):
                    step(c, e)
            pair_attention(CHUNKS, 0, "start")
            act.wait_ge(down_done, EXPERTS * CHUNKS)
            act.wait_ge(gt_ready, CHUNKS - 1)
            a.activation(o_th[:, :], O, ACT.Tanh, scale=0.5).then_inc(oth_ready, 1)

        @block.vector
        def _(dve):
            v = nc.vector
            n_self = [0]

            def link(ins):
                n_self[0] += 1
                ins.then_inc(dve_self, 1)
                dve.wait_ge(dve_self, n_self[0])

            def rsqrt_seed(a_, at):
                at = (slice(None), *at)
                v.tensor_scalar(half_a[at], a_, -0.5, None, ALU.mult)
                link(v.tensor_scalar(seed[at], a_.bitcast(i32), 1, None, ALU.logical_shift_right))
                return v.tensor_scalar(seed[at], seed[at], -1.0, RSQRT_MAGIC, ALU.mult, ALU.add)

            v.memset(scratch_dve[:, 0:1], 0.0).then_inc(k_lo_ready, 1)
            v.memset(scratch_dve[:, 1:2], 0.0).then_inc(v_lo_ready, 1)
            v.memset(scratch_dve[:, 2:3], 0.0).then_inc(gate0_ready, 1)

            def row_statistics(t):
                dve.wait_ge(x_in[t // CT], 16)
                return v.bn_stats(stats[:, t, :], x_sb[:, t, :])

            def both_scales(t0, t1, beside=()):
                r, beside = slice(t0, t1), iter(beside)

                def between():
                    for t in beside:
                        row_statistics(t).then_inc(stats0_ready, 1)
                        break

                for t in range(t0, t1):
                    ins = v.bn_aggr(mv[:, t, :], stats[:, t, :])
                link(ins)
                link(v.tensor_scalar(rs_arg[:, 0, r], mv[:, r, 1], EPS, None, ALU.add))
                link(v.scalar_tensor_tensor(rs_arg[:, 1, r], rs_arg[:, 0, r], EPS, mv[:, r, 1],
                                            ALU.mult, ALU.add))
                link(rsqrt_seed(rs_arg[:, :, r], (slice(0, 2), r)))
                src = seed[:, :, r].bitcast(f32)
                for k in range(3):
                    between()
                    link(v.tensor_tensor(newt[:, :, r], src, src, ALU.mult))
                    between()
                    link(v.tensor_tensor(newt2[:, :, r], newt[:, :, r], half_a[:, :, r], ALU.mult))
                    between()
                    link(v.scalar_tensor_tensor(rs[:, :, r], newt2[:, :, r], 1.5, src, ALU.add,
                                                ALU.mult))
                    src = rs[:, :, r]
                v.scalar_tensor_tensor(hz_bias[:, r], mv[:, r, 0], -1.0, rs[:, 1, r], ALU.mult,
                                       ALU.mult).then_inc(scales_ready, 1)

            def norm(c):
                for t in range(c * CT, (c + 1) * CT):
                    v.tensor_scalar(xn[:, t, :], x_sb[:, t, :], mv[:, t, 0:1], rs[:, 0, t:t + 1],
                                    ALU.subtract, ALU.mult).then_inc(xn_ready, 1)

            def second_norm(c):
                for t in range(c * CT, (c + 1) * CT):
                    ins = v.tensor_scalar(hz[:, t, :], x_sb[:, t, :], mv[:, t, 0:1],
                                          rs[:, 1, t:t + 1], ALU.subtract, ALU.mult)
                ins.then_inc(hz_ready, 1)

            def x_lo(c):
                dve.wait_ge(xt_hi_ready, c + 1)
                v.tensor_tensor(xT_lo[:, chunk(c)], T0, xT_hi[:, chunk(c)],
                                ALU.subtract).then_inc(xt_lo_ready, 1)

            def h_hi(c):
                dve.wait_ge(h32_ready, c + 1)
                v.tensor_copy(hT_hi[:, chunk(c)], hT32[:, c % 2, :]).then_inc(h_hi_ready, 1)

            def k_and_v_lo(c):
                dve.wait_ge(k_hi_ready, c + 1)
                v.tensor_tensor(kT_lo[:, chunk(c)], O, kT_hi[:, chunk(c)],
                                ALU.subtract).then_inc(k_lo_ready, 1)
                dve.wait_ge(v_hi_ready, c + 1)
                v.scalar_tensor_tensor(v_lo[:, ds(c * CT, CT), :], tiles_of(X), NORM_FACT,
                                       v_hi[:, ds(c * CT, CT), :], ALU.mult,
                                       ALU.subtract).then_inc(v_lo_ready, 1)

            def ffn_out(c):
                dve.wait_ge(fc2_done, c + 1)
                dve.wait_ge(xnb_ready, c + 1)
                dve.wait_ge(gate0_ready, c + 1)
                v.scalar_tensor_tensor(tiles_of(u0[:, :]), tiles_of(FC2_BANK[c]), 0.5,
                                       xnb[:, ds(c * CT, CT), :], ALU.mult, ALU.add).then_inc(u_ready, 1)

            for t in range(CT):
                ins = row_statistics(t)
            link(ins)
            both_scales(0, CT)
            norm(0)
            dve.wait_ge(A_hi_ready, 1)
            v.tensor_tensor(A_lo[:, :], SH[0][:, 0:P], A_hi[:, :], ALU.subtract).then_inc(A_lo_ready, 1)
            dve.wait_ge(ffn1_in, 32)
            v.scalar_tensor_tensor(fc1_w[:, :], q1_sb[:, :], -ZERO_POINT, s1_sb[:, :], ALU.add,
                                   ALU.mult).then_inc(fc1_ready, 1)
            for t in range(CT, 2 * CT):
                row_statistics(t).then_inc(stats0_ready, 1)
            x_lo(0)
            h_hi(0)
            dve.wait_ge(stats0_ready, CT)
            both_scales(CT, 2 * CT, range(2 * CT, 2 * CT + BESIDE))
            norm(1)
            second_norm(1)
            k_and_v_lo(0)
            x_lo(1)
            h_hi(1)
            for t in range(2 * CT + BESIDE, TILES):
                row_statistics(t).then_inc(stats0_ready, 1)
            dve.wait_ge(stats0_ready, TILES - CT)
            both_scales(2 * CT, TILES)
            for c in range(CHUNKS - 1):
                if c >= 1:
                    x_lo(c + 1)
                    h_hi(c + 1)
                ffn_out(c)
                if c == 0:
                    norm(2)
                    second_norm(2)
                k_and_v_lo(c + 1)
                if c == 0:
                    norm(3)

            def row_max(t, j):
                dve.wait_ge(s_done, t + 1)
                v.tensor_reduce(neg_max[:, ds(t, 1)], S[1 - j][:, :], AX.X, ALU.max,
                                negate=True).then_inc(max_ready, 1)

            def split_lo(t, j):
                dve.wait_ge(exp_done, t + 1)
                v.reciprocal(row_inv[:, ds(t, 1)], row_sum[:, ds(t, 1)])
                for h in range(2):
                    r = slice(h * CHUNK, (h + 1) * CHUNK)
                    dve.wait_ge(pt_hi_ready, 2 * t + h + 1)
                    v.tensor_tensor(pT_lo[:, j, r], T[h], pT_hi[:, j, r],
                                    ALU.subtract).then_inc(pt_lo_ready, 1)

            def gated_rows(t, j):
                dve.wait_ge(o_done, t + 1)
                v.scalar_tensor_tensor(sg0[:, j:j + 1, :], O[:, 0:P].unsqueeze(1),
                                       row_inv[:, ds(t, 1)], gate0[:, ds(t, 1), :],
                                       ALU.mult, ALU.mult).then_inc(o_read, 1)

            def statistics(t):
                dve.wait_ge(x1_ready, t + 1)
                v.bn_stats(stats1[:, ds(t, 1), :].rearrange("p a b -> p (a b)"),
                           x1[:, ds(t, 1), :].rearrange("p a b -> p (a b)")).then_inc(stats_ready, 1)

            def layer1_scale(b):
                r = slice(*GROUPS[b])
                dve.wait_ge(stats_ready, GROUPS[b][1])
                for t in range(*GROUPS[b]):
                    ins = v.bn_aggr(mv1[:, t, :], stats1[:, t, :])
                link(ins)
                link(v.tensor_scalar(rs1_arg[:, r], mv1[:, r, 1], EPS, None, ALU.add))
                rsqrt_seed(rs1_arg[:, r], (0, r)).then_inc(seed_ready, 1)

            def layer1_columns(c):
                dve.wait_ge(x1t_hi, c + 1)
                v.tensor_tensor(x1T_lo[:, chunk(c)], X, x1T_hi[:, chunk(c)],
                                ALU.subtract).then_inc(x1t_lo, 1)

            def body(t, j):
                row_max(t + 1, 1 - j)
                if not isinstance(t, int) or t >= 2:
                    statistics(t - 2)
                split_lo(t, j)
                if isinstance(t, int) and t == BT + 1:
                    layer1_scale(0)
                if not isinstance(t, int) or t >= 1:
                    gated_rows(t - 1, 1 - j)

            def read_logits(read):
                v.tensor_copy(logits[:, :, :], X[:, 0:BT * EXPERTS].rearrange("p (t e) -> p t e", e=EXPERTS))\
                    .then_inc(read, 1)

            def top(first_or_second):
                lg, l2 = logits[:, :, :], logits2[:, :, :]
                rank_b = rank[:, :].unsqueeze(1).broadcast_to(BE)
                src, value, one_hot = ((lg, top1, first), (l2, top2, second))[first_or_second]
                link(v.tensor_reduce(value[:, :], src, AX.X, ALU.max))
                link(v.tensor_tensor(equal[:, :, :], src, bc(value[:, :], EXPERTS), ALU.is_equal))
                link(v.tensor_tensor(ranked[:, :, :], equal[:, :, :], rank_b, ALU.mult))
                link(v.tensor_reduce(best[:, :], ranked[:, :, :], AX.X, ALU.max))
                link(v.tensor_tensor(one_hot[:, :, :], ranked[:, :, :], bc(best[:, :], EXPERTS),
                                     ALU.is_equal))
                if one_hot is first:
                    link(v.scalar_tensor_tensor(l2, first[:, :, :], LOWEST, lg, ALU.mult, ALU.add))
                else:
                    v.tensor_tensor(gap[:, :], top2[:, :], top1[:, :], ALU.subtract).then_inc(gap_ready, 1)

            def weights_of_two(b):
                dve.wait_ge(egap_ready, b + 1)
                link(v.tensor_scalar(wden[:, :], e_gap[:, :], 1.0, None, ALU.add))
                link(v.reciprocal(wtop1[:, :], wden[:, :]))
                link(v.tensor_tensor(wtop2[:, :], wtop1[:, :], e_gap[:, :], ALU.mult))
                v.tensor_tensor(first[:, :, :], first[:, :, :], bc(wtop1[:, :], EXPERTS), ALU.mult)
                link(v.tensor_tensor(second[:, :, :], second[:, :, :], bc(wtop2[:, :], EXPERTS), ALU.mult))
                link(v.tensor_tensor(wrow[:, :, :], first[:, :, :], second[:, :, :], ALU.add))
                hi = w16[:, b * BT:(b + 1) * BT, 0:EXPERTS]
                link(v.tensor_copy(hi, wrow[:, :, :]))
                v.tensor_tensor(w16[:, b * BT:(b + 1) * BT, EXPERTS:2 * EXPERTS], wrow[:, :, :], hi,
                                ALU.subtract).then_inc(w16_ready, 1)

            row_max(0, 0)
            row_max(1, 1)
            ffn_out(CHUNKS - 1)
            dve.wait_ge(gate0_ready, CHUNKS)
            split_lo(0, 0)
            body(1, 1)
            with dve.Fori(1, BT // 2) as half:
                for j in range(2):
                    body(2 * half + j, j)
            for t in range(BT, TILES - 1):
                if t == TILES - CT + 1:
                    dve.wait_ge(gate3_ready, 1)
                if t in (BT + 5, BT + 6):
                    layer1_columns(t - BT - 5)
                body(t, t % 2)

            def clip_gate(c, e):
                n = EXPERTS * c + e
                dve.wait_ge(gb_ready, n + 1)
                v.tensor_scalar(g_c[:, e % 2, :], g_c[:, e % 2, :], LIMIT, None,
                                ALU.min).then_inc(gc_ready, 1)

            def clip_up(c, e):
                n = EXPERTS * c + e
                dve.wait_ge(ub_ready, n + 1)
                if at_least(c, 1) or e >= 2:
                    dve.wait_ge(act_ready, n - 1)
                v.tensor_scalar(u_c[:, e % 2, :], u_b[:, e % 2, :], LIMIT + 1.0, 1.0 - LIMIT,
                                ALU.min, ALU.max).then_inc(uc_ready, 1)

            def gated(c, e):
                n = EXPERTS * c + e
                dve.wait_ge(gs_ready, n + 1)
                v.scalar_tensor_tensor(glu[:, e % 2, :], g_s[:, e % 2, :], 1.0, g_c[:, e % 2, :],
                                       ALU.add, ALU.mult).then_inc(glu_ready, 1)

            def wait_weights(c, e):
                if by_dram(c, e):
                    first_load = EXPERTS * BY_DRAM[0] + BY_DRAM[1]
                    first_load += (e - first_load) % SLOTS
                    dve.wait_ge(wb_in[e % SLOTS], 16 * (2 * c + e // SLOTS + 1 - first_load // SLOTS))
                else:
                    dve.wait_ge(wb_done, EXPERTS * c + e + 1)

            def weigh(c, e):
                n = EXPERTS * c + e
                dve.wait_ge(act_ready, n + 1)
                wait_weights(c, e)
                if at_least(c, 1) or e >= 2:
                    dve.wait_ge(down_done, n - 1)
                v.tensor_tensor(actw[:, e % 2, :], act32[:, e % 2, :], spread_of(c, e),
                                ALU.mult).then_inc(actw_ready, 1)

            def gate_columns(c):
                dve.wait_ge(oth_ready, c + 1)
                if at_least(c, 1):
                    dve.wait_ge(prod_ready, c)
                v.scalar_tensor_tensor(gT[:, :], o_th[:, :], 1.0, o_sum[:, :], ALU.add, ALU.mult)\
                    .then_inc(gt_ready, 1)

            def last_rows(c):
                dve.wait_ge(turned, c + 1)
                r = ds(c * CT, CT)
                v.tensor_tensor(x1[:, r, :], tiles_of(X), x1[:, r, :], ALU.add).then_inc(x2_ready, 1)

            def pair_attention(c, e, place):
                for n, kind, j, s in uses_at(c, e, place):
                    if kind == "columns":
                        layer1_columns(j)
                    if kind not in BY_DVE:
                        continue
                    dve.wait_ge(use_done, use_count(n))
                    if kind == "router":
                        read_logits(use_dve)
                    else:
                        dve.wait_ge(use_act, reads_until(use_of("dk", j))[0])
                        v.scalar_tensor_tensor(qk[j][:, s, :], X, vecs_sb[:, BQ:BQ + 1], dkT[:, j, :],
                                               ALU.add, ALU.mult).then_inc(use_dve, 1)

            def attend(j, s):
                for kind in (("headsum", j, s), ("dv", j)):
                    dve.wait_ge(use_act, reads_until(use_of(*kind))[0])
                v.scalar_tensor_tensor(adv[j][:, s, :], th[j][:, s, :], 1.0, dvT[:, j, :],
                                       ALU.add, ALU.mult).then_inc(adv_ready, 1)

            def step(c, e):
                pair_attention(c, e, "start")
                clip_gate(c, e)
                if exists(before(c, e, 1)[0]):
                    if not at_least(c, 2):
                        clip_up(*before(c, e, 1))
                    gated(*before(c, e, 1))
                pair_attention(c, e, "middle")
                if exists(before(c, e, 2)[0]):
                    weigh(*before(c, e, 2))
                if at_least(c, 2):
                    clip_up(c, e)
                for j, s in at(ADV_AT, c, e):
                    attend(j, s)
                if at_least(c, 1) and e == 3:
                    gate_columns(c - 1)
                if at_least(c, 2) and e == 0:
                    last_rows(c - 2)

            layer1_scale(1)
            dve.wait_ge(router_done, 1)
            read_logits(logits_read)
            dve.wait_ge(logits_read, 1)
            top(0)
            top(1)
            split_lo(TILES - 1, 1)
            gated_rows(TILES - 2, 0)
            statistics(TILES - 3)
            clip_gate(0, 0)
            weights_of_two(0)
            for e in range(1, EXPERTS):
                step(0, e)
                if e == 1:
                    dve.wait_ge(wt_done, 1)
                    v.tensor_copy(wT16[:, 0:KEYS], T0[0:2 * EXPERTS, :].bitcast(f16)).then_inc(wt_ready, 1)
                    gated_rows(TILES - 1, 1)
                    statistics(TILES - 2)
                if e == 3:
                    statistics(TILES - 1)
                    layer1_scale(2)
            for e in range(EXPERTS):
                step(1, e)
                if e == 2:
                    dve.wait_ge(use_dve, reads_until(use_of("router"))[1])
                    top(0)
                elif e == 3:
                    top(1)
                elif e == 4:
                    weights_of_two(1)
            clip_up(1, EXPERTS - 1)
            with dve.Fori(2, CHUNKS) as c:
                for e in range(EXPERTS):
                    step(c, e)
            last = (CHUNKS - 1, EXPERTS - 1)
            gated(*last)
            weigh(CHUNKS - 1, EXPERTS - 2)
            dve.wait_ge(glu_ready, EXPERTS * CHUNKS)
            slot = (EXPERTS - 1) % 2
            dve.wait_ge(actw_ready, EXPERTS * CHUNKS - 2)
            for h in HALVES:
                v.tensor_tensor(act32[:, slot, h], u_c[:, slot, h], glu[:, slot, h],
                                ALU.mult).then_inc(last_act_ready, 1)
            wait_weights(*last)
            dve.wait_ge(down_done, EXPERTS * CHUNKS - 2)
            for n, h in enumerate(HALVES):
                dve.wait_ge(last_act_ready, n + 1)
                v.tensor_tensor(actw[:, slot, h], act32[:, slot, h], spread_of(*last)[:, h],
                                ALU.mult).then_inc(actw_ready, 1)
            last_rows(CHUNKS - 2)
            dve.wait_ge(prod_ready, CHUNKS - 1)
            dve.wait_ge(turned, CHUNKS - 1)
            dve.wait_ge(oth_ready, CHUNKS)
            for h in HALVES:
                link(v.scalar_tensor_tensor(gT[:, h], o_th[:, h], 1.0, O[:, h], ALU.add, ALU.mult))
                v.tensor_tensor(prodT[:, h], gT[:, h], sT[:, CHUNK * (CHUNKS - 1) + h.start:
                                                          CHUNK * (CHUNKS - 1) + h.stop],
                                ALU.mult).then_inc(prod_ready, 1)
            for n, h in enumerate(HALVES):
                dve.wait_ge(turned, CHUNKS + n)
                r = half_tiles(n)
                v.tensor_tensor(x1[:, r, :], tiles_of(T[n][:, h]), x1[:, r, :],
                                ALU.add).then_inc(x2_ready, 1)

        @block.tensor
        def _(pe):
            mm = nc.tensor.matmul

            def three(o, l_hi, l_lo, r_hi, r_lo):
                mm(o, l_hi, r_hi, start=True, stop=False)
                mm(o, l_hi, r_lo, start=False, stop=False)
                return mm(o, l_lo, r_hi, start=False, stop=True)

            def turn_tiles(bank, src, first):
                for k in range(CT):
                    ins = nc.tensor.transpose(bank[:, k * P:(k + 1) * P], src[:, first + k, :], ident[:, :])
                return ins

            pe.wait_ge(w0_in, 16)
            mm(SH[0][:, 0:P], w0_sb[:, WK, :], w0_sb[:, WQ, :], start=True, stop=True).then_inc(A_ready, 1)

            def columns(c):
                pe.wait_ge(xn_ready, CT * (c + 1))
                if c:
                    pe.wait_ge(xt_lo_ready, c)
                turn_tiles(T0, xn, CT * c).then_inc(xt_done, 1)
                pe.wait_ge(hz_ready, c + 1)
                if c:
                    pe.wait_ge(h32_ready, c)
                turn_tiles(T1, hz, CT * c).then_inc(ht_done, 1)

            def k_and_v(c):
                pe.wait_ge(xt_lo_ready, c + 1)
                pe.wait_ge(k_lo_ready, c + 1)
                three(O, A_hi[:, :], A_lo[:, :], xT_hi[:, chunk(c)], xT_lo[:, chunk(c)])\
                    .then_inc(k_done, 1)
                pe.wait_ge(v_lo_ready, c + 1)
                for k in range(CT):
                    tok = slice(c * CHUNK + k * P, c * CHUNK + (k + 1) * P)
                    ins = three(X[:, k * P:(k + 1) * P], xT_hi[:, tok], xT_lo[:, tok],
                                wv_hi[:, :], wv_lo[:, :])
                ins.then_inc(v_done, 1)

            def fc1(c):
                pe.wait_ge(h_lo_ready, c + 1)
                for i, f in enumerate(F_ORDER):
                    w = slice(f * P, (f + 1) * P)
                    pe.wait_ge(y_ready, FB * c + i + 1)
                    if f == 0 and c:
                        pe.wait_ge(u_ready, c)
                    three(SH[f], fc1_hi[:, w], fc1_lo[:, w], hT_hi[:, chunk(c)],
                          hT_lo[:, chunk(c)]).then_inc(fc1_done, 1)

            def fc2(c, bank):
                pe.wait_ge(y_ready, FB * (c + 2))
                for k in range(CT):
                    for f in range(FB):
                        ins = mm(bank[:, k * P:(k + 1) * P], yT[:, f, k * P:(k + 1) * P], fc2_w[:, f, :],
                                 start=(f == 0), stop=(f == FB - 1))
                ins.then_inc(fc2_done, 1)

            def logit(t, j, b):
                if not isinstance(t, int) or t >= 2:
                    pe.wait_ge(exp_done, t - 1)
                q = ds(t * P, P)
                for h in range(2):
                    keys = slice(b * KEYS + h * CHUNK, b * KEYS + (h + 1) * CHUNK)
                    ins = three(S[1 - j][:, h * CHUNK:(h + 1) * CHUNK], xT_hi[:, q], xT_lo[:, q],
                                kT_hi[:, keys], kT_lo[:, keys])
                ins.then_inc(s_done, 1)

            def turn(t, j):
                pe.wait_ge(exp_done, t + 1)
                for h in range(2):
                    if not isinstance(t, int) or t >= 1:
                        pe.wait_ge(pt_lo_ready, 2 * t - 1 + h)
                    for k in range(CT):
                        at = h * CHUNK + k * P
                        ins = nc.tensor.transpose(T[h][:, k * P:(k + 1) * P], probs[:, j, at:at + P],
                                                  ident[:, :])
                    ins.then_inc(pt_done, 1)

            def weighted(t, j, b):
                if not isinstance(t, int) or t >= 1:
                    pe.wait_ge(o_read, t)
                for m in range(BT):
                    if m % CT == 0:
                        pe.wait_ge(pt_lo_ready, 2 * t + m // CT + 1)
                    at, vt = slice(m * P, (m + 1) * P), b * BT + m
                    for n, (l, r) in enumerate(((pT_hi, v_hi), (pT_hi, v_lo), (pT_lo, v_hi))):
                        ins = mm(O[:, 0:P], l[:, j, at], r[:, vt, :], start=(m == 0 and n == 0),
                                 stop=(m == BT - 1 and n == 2))
                ins.then_inc(o_done, 1)

            def body(t, j, b, b_logit):
                turn(t, j)
                if not isinstance(t, int) or t >= 1:
                    weighted(t - 1, 1 - j, b)
                if b_logit is not None:
                    logit(t + 2, j, b_logit)

            pe.wait_ge(consts_ready, 1)
            columns(0)
            for ready in (A_lo_ready, wv_ready):
                pe.wait_ge(ready, 1)
            k_and_v(0)
            pe.wait_ge(fc1_lo_ready, 1)
            for c in range(CHUNKS):
                fc1(c)
                if c + 1 < CHUNKS:
                    columns(c + 1)
                else:
                    pe.wait_ge(y_ready, FB * CHUNKS + 3)
                    logit(0, 0, 0)
                    pe.wait_ge(y_ready, FB * (CHUNKS + 1))
                    logit(1, 1, 0)
                    pe.wait_ge(v_lo_ready, CHUNKS + 1)
                if c == 0:
                    pe.wait_ge(fc2_ready, 2)
                fc2(c, FC2_BANK[c])
                if c + 1 < CHUNKS:
                    k_and_v(c + 1)
            turn(0, 0)
            logit(2, 0, 0)
            pe.wait_ge(k_lo_ready, CHUNKS + 1)
            body(1, 1, 0, 0)
            with pe.Fori(1, BT // 2 - 1) as half:
                for j in range(2):
                    body(2 * half + j, j, 0, 0)
            body(BT - 2, 0, 0, 1)
            body(BT - 1, 1, 0, 1)
            body(BT, 0, 0, 1)
            body(BT + 1, 1, 1, 1)

            def layer1_columns(c):
                for half_done in (x1n_pool, x1n_act):
                    pe.wait_ge(half_done, CT // 2 * (c + 1))
                if c == 0:
                    pe.wait_ge(u_ready, CHUNKS)
                elif c == 1:
                    pe.wait_ge(x1t_lo, 1)
                turn_tiles(X, x1n, CT * c).then_inc(x1t_done, 1)

            def router(b):
                cols = slice(4 * P, 4 * P + EXPERTS)
                for k in range(BT):
                    tok = slice((b * BT + k) * P, (b * BT + k + 1) * P)
                    ins = three(X[:, k * EXPERTS:(k + 1) * EXPERTS], x1T_hi[:, tok], x1T_lo[:, tok],
                                w1_hi[:, cols], w1_lo[:, cols])
                return ins

            def weight_columns(bank, b):
                for k in range(BT):
                    ins = nc.tensor.transpose(bank[0:2 * EXPERTS, :].bitcast(f16)[:, k * P:(k + 1) * P],
                                              w16[:, b * BT + k, :], ident16[:, :])
                return ins

            for t in range(BT + 2, TILES - 2):
                turn(t, t % 2)
                weighted(t - 1, 1 - t % 2, 1)
                if t in (BT + 4, BT + 5):
                    layer1_columns(t - BT - 4)
                logit(t + 2, t % 2, 1)
            turn(TILES - 2, 0)
            weighted(TILES - 3, 1, 1)
            pe.wait_ge(l1w_ready, 1 + 2 * EXPERTS)
            pe.wait_ge(x1t_lo, 2)
            router(0).then_inc(router_done, 1)
            turn(TILES - 1, 1)
            weighted(TILES - 2, 0, 1)

            def up_side(c, e):
                n, cols = EXPERTS * c + e, chunk(c)
                late = at_least(c, 1) or e >= 2
                if late:
                    pe.wait_ge(gb_ready, n - 1)
                three(SH[e % 2], gup_hi[:, e, 0, :], gup_lo[:, e, 0, :], x1T_hi[:, cols],
                      x1T_lo[:, cols]).then_inc(gate_done, 1)
                if late:
                    pe.wait_ge(ub_ready, n - 1)
                three(SH[2 + e % 2], gup_hi[:, e, 1, :], gup_lo[:, e, 1, :], x1T_hi[:, cols],
                      x1T_lo[:, cols]).then_inc(up_done, 1)

            def spread(c, e):
                n = EXPERTS * c + e
                if n >= 2:
                    pe.wait_ge(actw_ready, n - 1)
                mm(T[e % 2], sel16[:, e, :], wT16[:, chunk(c)], start=True, stop=True).then_inc(wb_done, 1)

            def halved_weights(bank, c):
                return mm(bank[0:EXPERTS, :], sel16[:, :, 0], wT16[:, chunk(c)], start=True, stop=True)

            def down_side(c, e):
                n = EXPERTS * c + e
                if e == 0:
                    if at_least(c, 1):
                        pe.wait_ge(sum_read, c)
                    else:
                        pe.wait_ge(o_read, TILES)
                pe.wait_ge(actw_ready, n + 1)
                mm(O, down_sb[:, e, :], actw[:, e % 2, :], start=(e == 0),
                   stop=(e == EXPERTS - 1)).then_inc(down_done, 1)
                if e == 0:
                    mm(O, db_hi[:, :], wT16[:, chunk(c)], start=False, stop=False)
                    mm(O, db_lo[:, :], wT16[:, chunk(c)], start=False, stop=False)

            def turn_back(c):
                pe.wait_ge(prod_ready, c + 1)
                if at_least(c, 1):
                    pe.wait_ge(x2_ready, c)
                for k in range(CT):
                    ins = nc.tensor.transpose(X[:, k * P:(k + 1) * P], prodT[:, k * P:(k + 1) * P],
                                              ident[:, :])
                ins.then_inc(turned, 1)

            def proj(i, c, start=True, stop=True, neg=False):
                w = slice(i * P, (i + 1) * P) if not neg else slice((i - IK) * P, (i - IK + 1) * P)
                w_hi, w_lo = (wneg_hi, wneg_lo) if neg else (w1_hi, w1_lo)
                mm(X, w_hi[:, w], x1T_hi[:, chunk(c)], start=start, stop=False)
                mm(X, w_hi[:, w], x1T_lo[:, chunk(c)], start=False, stop=False)
                return mm(X, w_lo[:, w], x1T_hi[:, chunk(c)], start=False, stop=stop)

            def pair_attention(c, e, place):
                for n, kind, j, s in uses_at(c, e, place):
                    if c == CHUNKS:
                        pe.wait_ge(halved_last, 1)
                    elif n:
                        wait_read(pe, n - 1)
                    else:
                        pe.wait_ge(logits_read, 1)
                    if kind == "columns":
                        layer1_columns(j)
                        continue
                    if kind == "rows":
                        turn_back(0)
                        continue
                    if kind == "router":
                        ins = router(1)
                    elif kind == "weights":
                        pe.wait_ge(w16_ready, 2)
                        ins = weight_columns(X, 1)
                    elif kind == "halved":
                        ins = halved_weights(X, s)
                    elif kind in ("dk", "dv"):
                        i = IK if kind == "dk" else IV
                        proj(i, j, stop=False)
                        ins = proj(i, 2 + j, start=False, neg=True)
                    elif kind == "v1":
                        ins = proj(IV, 2 + j)
                    elif kind == "q":
                        ins = proj(IQ, j + 2 * s)
                    elif kind == "headsum":
                        pe.wait_ge(qk_lo_ready, SPLIT_ORDER.index((j, s)) + 1)
                        mm(X, headsum16[:, :], qk_hi[:, j, s, :], start=True, stop=False)
                        ins = mm(X, headsum16[:, :], qk_lo[:, j, s, :], start=False, stop=True)
                    else:
                        pe.wait_ge(ctx_ready, CTX_ORDER.index((j, s)) + 1)
                        ins = mm(bank_of_out(c), w1_sb[:, OUT * P:OUT * P + P], ctxT[j][:, s, :], start=True,
                                 stop=True)
                    ins.then_inc(use_done, 1)

            def step(c, e):
                pair_attention(c, e, "start")
                up_side(c, e)
                pair_attention(c, e, "middle")
                if exists(before(c, e, 3)[0]):
                    down_side(*before(c, e, 3))
                if exists(before(c, e, 1)[0]) and not by_dram(*before(c, e, 1)):
                    spread(*before(c, e, 1))

            pe.wait_ge(exp_done, TILES)
            up_side(0, 0)
            up_side(0, 1)
            up_side(0, 2)
            weighted(TILES - 1, 1, 1)
            up_side(0, 3)
            pe.wait_ge(w16_ready, 1)
            weight_columns(T0, 0).then_inc(wt_done, 1)
            pair_attention(0, 3, "start")
            pe.wait_ge(wt_ready, 1)
            spread(0, 0)
            spread(0, 1)
            up_side(0, 4)
            down_side(0, 0)
            spread(0, 2)
            pair_attention(0, 4, "middle")
            down_side(0, 1)
            spread(0, 3)
            for e in range(5, EXPERTS):
                step(0, e)
            for e in range(EXPERTS):
                step(1, e)
            halved_weights(T0, CHUNKS - 1).then_inc(halved_done, 1)
            with pe.Fori(2, CHUNKS) as c:
                for e in range(EXPERTS):
                    step(c, e)
                    if e == 5:
                        turn_back(c - 1)
            pair_attention(CHUNKS, 0, "start")
            for e in (EXPERTS - 3, EXPERTS - 2):
                down_side(CHUNKS - 1, e)
            for n, h in enumerate(HALVES):
                pe.wait_ge(actw_ready, EXPERTS * CHUNKS + n)
                ins = mm(O[:, h], down_sb[:, EXPERTS - 1, :], actw[:, (EXPERTS - 1) % 2, h],
                         start=False, stop=(n == 1))
            ins.then_inc(down_done, 1)
            by_act, _ = reads_until(len(USES) - 1)
            pe.wait_ge(use_act, by_act)
            for n, h in enumerate(HALVES):
                pe.wait_ge(prod_ready, CHUNKS + n)
                for k in range(h.start, h.stop, P):
                    ins = nc.tensor.transpose(T[n][:, k:k + P], prodT[:, k:k + P], ident[:, :])
                ins.then_inc(turned, 1)


def kernel(**inputs):
    import numpy as np
    import concourse.bacc as bacc
    from concourse.bass_utils import run_bass_kernel_spmd

    a = {k: np.asarray(v) for k, v in inputs.items()}
    in_w = a["L1_attn_in_proj_weight"].reshape(HEADS, 3, HD, P).transpose(1, 0, 2, 3).reshape(3, P, P)
    in_b = a["L1_attn_in_proj_bias"].reshape(HEADS, 3, HD).transpose(1, 0, 2).reshape(3, P)
    gup = a["L1_ffn_gate_up_proj"].reshape(EXPERTS, P, P, 2).transpose(1, 0, 3, 2)
    gub = a["L1_ffn_gate_up_proj_bias"].reshape(EXPERTS, P, 2)
    arrays = {
        "x": a["L0_attn_x"].reshape(TOKENS, P),
        "w0": np.stack([a["L0_attn_Wq"], a["L0_attn_Wk"], a["L0_attn_Wv"].T], axis=1),
        "w1s": np.concatenate([in_w[0].T, in_w[1].T, in_w[2].T, a["L1_attn_out_proj_weight"].T,
                               a["L1_ffn_router_weight"]], axis=1),
        "vecs": np.stack([a["L0_ffn_ln_gamma"], a["L0_ffn_ln_beta"],
                          *a["L0_ffn_fc1_bias"].reshape(FB, P), in_b[0], in_b[2],
                          a["L1_attn_out_proj_bias"], *gub[:, :, 0], *gub[:, :, 1]], axis=1),
        "q1": a["L0_ffn_fc1_q"],
        "q2": a["L0_ffn_fc2_q"].reshape(FB, P, P).transpose(1, 0, 2),
        "s1": a["L0_ffn_fc1_scales"].reshape(FFN),
        "s2": a["L0_ffn_fc2_scales"],
        "b2": a["L0_ffn_fc2_bias"],
        "gup": gup,
        "down": a["L1_ffn_down_proj"].transpose(1, 0, 2),
        "db": np.concatenate([a["L1_ffn_down_proj_bias"]] * 2, axis=0),
    }
    nc = bacc.Bacc("TRN2", target_bir_lowering=False, num_devices=1)
    arrays = {k: np.ascontiguousarray(v) for k, v in arrays.items()}
    args = [nc.dram_tensor(k, v.shape, mybir.dt.from_np(v.dtype), kind="ExternalInput").ap()
            for k, v in arrays.items()]
    out = nc.dram_tensor("out", (TOKENS, P), mybir.dt.float32, kind="ExternalOutput").ap()
    build(nc, *args, out)
    r = run_bass_kernel_spmd(nc, [arrays], core_ids=[0])
    return r.results[0]["out"].reshape(BATCHES, KEYS, P)
```
